# Optimizing a Trainium2 kernel written in Bass

```python
import numpy as np
import jax
import jax.numpy as jnp

def _softmax(x, axis=-1):
    return jax.nn.softmax(x, axis=axis)

def _gelu(x):
    return jax.nn.gelu(x, approximate=True)

def _silu(x):
    return jax.nn.silu(x)

def _sigmoid(x):
    return jax.nn.sigmoid(x)

def _layernorm(x, axis=-1, eps=1e-05):
    m = jnp.mean(x, axis=axis, keepdims=True)
    v = jnp.var(x, axis=axis, keepdims=True)
    return (x - m) / jnp.sqrt(v + eps)

def _scatter_add(tgt, idx, src, axis=0):
    return tgt.at[idx].add(src)

def _segment_sum(src, seg, n):
    return jax.ops.segment_sum(src, seg, n)
kernel_name = 'mk_prb_d2_jaxref_r8_be8913'

def setup_inputs(seed: int=0):
    np.random.seed(seed)
    _w = jnp.asarray

    def _L0_attn_setup():
        import jax, jax.numpy as jnp
        import numpy as np
        B, S, E, H, D = (4, 256, 128, 16, 64)

        def _large_negative_number(dtype):
            return jnp.asarray(-0.7 * jnp.finfo(dtype).max, dtype=dtype)
        key = jax.random.key(seed)
        k1, k2, k3 = jax.random.split(key, 3)
        x = jax.random.normal(k1, (B, S, E), dtype=jnp.float32)
        qkv_w = jax.random.normal(k2, (E, H, 3 * D), dtype=jnp.float32) * (1.0 / np.sqrt(E))
        qkv_b = jnp.zeros((H, 3 * D), dtype=jnp.float32)
        out_w = jax.random.normal(k3, (H, D, E), dtype=jnp.float32) * (1.0 / np.sqrt(H * D))
        out_b = jnp.zeros((E,), dtype=jnp.float32)
        return {'x': x, 'qkv_w': qkv_w, 'qkv_b': qkv_b, 'out_w': out_w, 'out_b': out_b}
    _L0_attn_in = _L0_attn_setup()

    def _L0_ffn_setup():
        import jax, jax.numpy as jnp
        import numpy as np
        DIM = 128
        HIDDEN = 384
        SCALE = 1.0 / 127.0

        def _dequant(w_int, dtype):
            return w_int.astype(dtype) * jnp.asarray(SCALE, dtype)
        key = jax.random.key(seed)
        k_x, k_g, k_u, k_d = jax.random.split(key, 4)
        x = jax.random.normal(k_x, (4, 256, DIM), dtype=jnp.float32)
        w_gate = jax.random.randint(k_g, (HIDDEN, DIM), -127, 128, dtype=jnp.int32)
        w_up = jax.random.randint(k_u, (HIDDEN, DIM), -127, 128, dtype=jnp.int32)
        w_down = jax.random.randint(k_d, (DIM, HIDDEN), -127, 128, dtype=jnp.int32)
        return {'x': x, 'w_gate': w_gate, 'w_up': w_up, 'w_down': w_down}
    _L0_ffn_in = _L0_ffn_setup()

    def _L1_attn_setup():
        import jax, jax.numpy as jnp
        import numpy as np
        SLEN, BSZ, IN_DIM = (256, 8, 128)
        H, D = (16, 64)
        LN_EPS = 1e-05

        def elu_p1(x):
            return jax.nn.elu(x) + 1.0

        def sum_norm(x):
            return x / jnp.sum(x, axis=-1, keepdims=True)

        def _forward(x, ln_w, ln_b, w_slow, w_out):
            slen, bsz, in_dim = x.shape
            mu = jnp.mean(x, axis=-1, keepdims=True)
            var = jnp.mean(jnp.square(x - mu), axis=-1, keepdims=True)
            h = (x - mu) * jax.lax.rsqrt(var + LN_EPS) * ln_w + ln_b
            qkvb = (h @ w_slow).reshape(slen, bsz, H, 3 * D + 1)
            q, k, v, beta = jnp.split(qkvb, [D, 2 * D, 3 * D], axis=-1)
            beta = jax.nn.sigmoid(beta)
            q = sum_norm(elu_p1(q))
            k = sum_norm(elu_p1(k))
            W0 = jnp.zeros((bsz, H, D, D), x.dtype)

            def step(W, qkvb_t):
                q_t, k_t, v_t, b_t = qkvb_t
                v_old = jnp.einsum('bhij,bhj->bhi', W, k_t)
                delta = b_t * (v_t - v_old)
                W_new = W + delta[..., :, None] * k_t[..., None, :]
                out_t = jnp.einsum('bhij,bhj->bhi', W_new, q_t)
                return (W_new, out_t)
            _, out = jax.lax.scan(step, W0, (q, k, v, beta))
            out = out.reshape(slen, bsz, H * D) @ w_out
            return x + out
        key = jax.random.key(seed)
        k1, k2, k3, k4, k5 = jax.random.split(key, 5)
        x = jax.random.normal(k1, (SLEN, BSZ, IN_DIM), dtype=jnp.float32)
        ln_w = jnp.ones((IN_DIM,), jnp.float32) + 0.02 * jax.random.normal(k2, (IN_DIM,), jnp.float32)
        ln_b = 0.02 * jax.random.normal(k3, (IN_DIM,), jnp.float32)
        w_slow = jax.random.normal(k4, (IN_DIM, H * (3 * D + 1)), jnp.float32) / np.sqrt(IN_DIM)
        w_out = jax.random.normal(k5, (H * D, IN_DIM), jnp.float32) / np.sqrt(H * D)
        return {'x': x, 'ln_w': ln_w, 'ln_b': ln_b, 'w_slow': w_slow, 'w_out': w_out}
    _L1_attn_in = _L1_attn_setup()

    def _L1_ffn_setup():
        import jax, jax.numpy as jnp
        import numpy as np
        E = 8
        D = 128
        H = 256
        TOP_K = 2
        key = jax.random.key(seed)
        k_x, k_g, k_w1, k_w2 = jax.random.split(key, 4)
        B, S = (4, 256)
        inp = {'input': jax.random.normal(k_x, (B, S, D), dtype=jnp.float32), 'Wg': jax.random.normal(k_g, (D, E), dtype=jnp.float32) * 0.02, 'W1': jax.random.normal(k_w1, (E, D, H), dtype=jnp.float32) * 0.02, 'b1': jnp.zeros((E, H), dtype=jnp.float32), 'W2': jax.random.normal(k_w2, (E, H, D), dtype=jnp.float32) * 0.02, 'b2': jnp.zeros((E, D), dtype=jnp.float32)}
        return inp
    _L1_ffn_in = _L1_ffn_setup()
    _d = {'L0_attn_x': _L0_attn_in['x'], 'L0_attn_qkv_w': _L0_attn_in['qkv_w'], 'L0_attn_qkv_b': _L0_attn_in['qkv_b'], 'L0_attn_out_w': _L0_attn_in['out_w'], 'L0_attn_out_b': _L0_attn_in['out_b'], 'L0_ffn_w_gate': _L0_ffn_in['w_gate'], 'L0_ffn_w_up': _L0_ffn_in['w_up'], 'L0_ffn_w_down': _L0_ffn_in['w_down'], 'L1_attn_ln_w': _L1_attn_in['ln_w'], 'L1_attn_ln_b': _L1_attn_in['ln_b'], 'L1_attn_w_slow': _L1_attn_in['w_slow'], 'L1_attn_w_out': _L1_attn_in['w_out'], 'L1_ffn_Wg': _L1_ffn_in['Wg'], 'L1_ffn_W1': _L1_ffn_in['W1'], 'L1_ffn_b1': _L1_ffn_in['b1'], 'L1_ffn_W2': _L1_ffn_in['W2'], 'L1_ffn_b2': _L1_ffn_in['b2']}
    _x0 = _d['L0_attn_x']
    _d['L0_attn_x'] = jax.random.normal(jax.random.fold_in(jax.random.key(seed), 1), (4, 1024, 128), dtype=_x0.dtype)
    del _x0
    return _d

def reference(L0_attn_x, L0_attn_qkv_w, L0_attn_qkv_b, L0_attn_out_w, L0_attn_out_b, L0_ffn_w_gate, L0_ffn_w_up, L0_ffn_w_down, L1_attn_ln_w, L1_attn_ln_b, L1_attn_w_slow, L1_attn_w_out, L1_ffn_Wg, L1_ffn_W1, L1_ffn_b1, L1_ffn_W2, L1_ffn_b2):

    def _L0_attn_ref(x, qkv_w, qkv_b, out_w, out_b):
        import jax, jax.numpy as jnp
        import numpy as np
        B, S, E, H, D = (4, 256, 128, 16, 64)

        def _large_negative_number(dtype):
            return jnp.asarray(-0.7 * jnp.finfo(dtype).max, dtype=dtype)
        qkv = jnp.einsum('bse,ehd->bshd', x, qkv_w) + qkv_b
        q, k, v = jnp.split(qkv, 3, axis=-1)
        logits = jnp.einsum('bqhd,bkhd->bhqk', q, k)
        logits = logits / jnp.sqrt(jnp.asarray(q.shape[-1], logits.dtype))
        mask = jnp.tril(jnp.ones((q.shape[1], q.shape[1]), dtype=jnp.bool_))
        logits = jnp.where(mask, logits, _large_negative_number(logits.dtype))
        probs = jax.nn.softmax(logits, axis=-1)
        attn = jnp.einsum('bhqk,bkhd->bqhd', probs, v)
        return jnp.einsum('bqhd,hde->bqe', attn, out_w) + out_b

    def _L0_ffn_ref(x, w_gate, w_up, w_down):
        import jax, jax.numpy as jnp
        import numpy as np
        DIM = 128
        HIDDEN = 384
        SCALE = 1.0 / 127.0

        def _dequant(w_int, dtype):
            return w_int.astype(dtype) * jnp.asarray(SCALE, dtype)
        wg = _dequant(w_gate, x.dtype)
        wu = _dequant(w_up, x.dtype)
        wd = _dequant(w_down, x.dtype)
        gate = jnp.einsum('bsd,hd->bsh', x, wg)
        up = jnp.einsum('bsd,hd->bsh', x, wu)
        h = jax.nn.silu(gate) * up
        return jnp.einsum('bsh,dh->bsd', h, wd)

    def _L1_attn_ref(x, ln_w, ln_b, w_slow, w_out):
        import jax, jax.numpy as jnp
        import numpy as np
        SLEN, BSZ, IN_DIM = (256, 8, 128)
        H, D = (16, 64)
        LN_EPS = 1e-05

        def elu_p1(x):
            return jax.nn.elu(x) + 1.0

        def sum_norm(x):
            return x / jnp.sum(x, axis=-1, keepdims=True)

        def _forward(x, ln_w, ln_b, w_slow, w_out):
            slen, bsz, in_dim = x.shape
            mu = jnp.mean(x, axis=-1, keepdims=True)
            var = jnp.mean(jnp.square(x - mu), axis=-1, keepdims=True)
            h = (x - mu) * jax.lax.rsqrt(var + LN_EPS) * ln_w + ln_b
            qkvb = (h @ w_slow).reshape(slen, bsz, H, 3 * D + 1)
            q, k, v, beta = jnp.split(qkvb, [D, 2 * D, 3 * D], axis=-1)
            beta = jax.nn.sigmoid(beta)
            q = sum_norm(elu_p1(q))
            k = sum_norm(elu_p1(k))
            W0 = jnp.zeros((bsz, H, D, D), x.dtype)

            def step(W, qkvb_t):
                q_t, k_t, v_t, b_t = qkvb_t
                v_old = jnp.einsum('bhij,bhj->bhi', W, k_t)
                delta = b_t * (v_t - v_old)
                W_new = W + delta[..., :, None] * k_t[..., None, :]
                out_t = jnp.einsum('bhij,bhj->bhi', W_new, q_t)
                return (W_new, out_t)
            _, out = jax.lax.scan(step, W0, (q, k, v, beta))
            out = out.reshape(slen, bsz, H * D) @ w_out
            return x + out
        return _forward(x, ln_w, ln_b, w_slow, w_out)

    def _L1_ffn_ref(input, Wg, W1, b1, W2, b2):
        import jax, jax.numpy as jnp
        import numpy as np
        E = 8
        D = 128
        H = 256
        TOP_K = 2
        logits = jnp.einsum('bsd,de->bse', input, Wg)
        probs = jax.nn.softmax(logits, axis=-1)
        top_vals, top_idx = jax.lax.top_k(probs, TOP_K)
        top_vals = top_vals / jnp.sum(top_vals, axis=-1, keepdims=True)
        onehot = jax.nn.one_hot(top_idx, E, dtype=input.dtype)
        mask = jnp.sum(onehot, axis=2)
        scores = jnp.sum(onehot * top_vals[..., None], axis=2)
        xm = input[None] * jnp.moveaxis(mask, -1, 0)[..., None]
        h = jnp.einsum('ebsd,edh->ebsh', xm, W1) + b1[:, None, None, :]
        h = jax.nn.relu(h)
        y = jnp.einsum('ebsh,ehd->ebsd', h, W2) + b2[:, None, None, :]
        out = jnp.sum(y * jnp.moveaxis(scores, -1, 0)[..., None], axis=0)
        return out
    x = L0_attn_x
    xn = _layernorm(x, axis=-1)
    x = x + _L0_attn_ref(xn, L0_attn_qkv_w, L0_attn_qkv_b, L0_attn_out_w, L0_attn_out_b) + _L0_ffn_ref(xn, L0_ffn_w_gate, L0_ffn_w_up, L0_ffn_w_down)
    xn = _layernorm(x, axis=-1)
    x = x + _L1_attn_ref(xn, L1_attn_ln_w, L1_attn_ln_b, L1_attn_w_slow, L1_attn_w_out) + _L1_ffn_ref(xn, L1_ffn_Wg, L1_ffn_W1, L1_ffn_b1, L1_ffn_W2, L1_ffn_b2)
    return x

_drawn_inputs = setup_inputs


def setup_inputs(seed=0):
    import zlib

    import numpy as np

    out = dict(_drawn_inputs(seed))
    spreads = {'L0_attn_qkv_b': (0.0, 0.8),
     'L0_attn_out_b': (0.0, 2.0),
     'L1_ffn_b1': (0.0, 2.0),
     'L1_ffn_b2': (0.0, 2.0)}
    factors = {'L0_attn_qkv_w': 8.0,
     'L0_attn_out_w': 8.0,
     'L1_attn_ln_w': 200.0,
     'L1_attn_ln_b': 200.0,
     'L1_attn_w_slow': 8.0,
     'L1_attn_w_out': 8.0,
     'L1_ffn_Wg': 60.523,
     'L1_ffn_W1': 64.0,
     'L1_ffn_W2': 56.017}
    for name, (base, spread) in spreads.items():
        noise = np.random.default_rng([zlib.crc32(name.encode()), seed]).standard_normal(out[name].shape)
        drawn = base * np.exp(spread * noise) if base else spread * noise
        out[name] = jnp.asarray(drawn.astype(out[name].dtype))
    for name, factor in factors.items():
        out[name] = (out[name] * factor).astype(out[name].dtype)
    return out
```

```python
from contextlib import ExitStack

import concourse.bass as bass
from concourse import mybir

F32 = mybir.dt.float32
BF16 = mybir.dt.bfloat16
I32 = mybir.dt.int32
ALU = mybir.AluOpType
ACT = mybir.ActivationFunctionType
AX = mybir.AxisListType

P = 128
E = 128
B, S = 4, 1024
ROWS = S // P
H, D = 16, 64
PAIRS = H // 2
HID = 384
NHID = HID // P
X, XH, NXB = 8, 256, 2
TOP = 2
QG = 2
GB = ROWS // QG
EPS = 1e-5
SCALE = D ** -0.5
INT_SCALE = 1.0 / 127.0
MASKED = -0.7 * 3.4028234663852886e38
NEG = MASKED

SCORES = 2 * ROWS
FLIPS = GB + 2 * GB


def flips_before(qb):
    return qb if qb < GB else GB + 2 * (qb - GB)


def block_kernel(nc, x, qkv_w, qkv_b, out_w, out_b, w_gate, w_up, w_down, ln_w, ln_b, w_slow, w_out,
                 Wg, W1, b1, W2, b2, out):
    top = ExitStack()
    with top:
        def sem(name):
            return top.enter_context(nc.semaphore(name))

        def sbuf(name, shape, dt=F32, where=top):
            return where.enter_context(nc.sbuf_tensor(name, shape, dt))

        def psum(name, shape, dt=F32):
            return top.enter_context(nc.psum_tensor(name, shape, dt))

        pair = [psum("pair0", [P, 1024]), psum("pair1", [P, 1024])]
        flip = [psum("flip0", [P, 512]), psum("flip1", [P, 512])]
        accum = psum("accum", [P, 512])
        misc = psum("misc", [P, 512])

        x1 = sbuf("x1", [P, B, ROWS, E])
        ident = sbuf("ident", [P, P])
        columns = sbuf("columns", [P, 34])
        bq8, bk = columns[:, 0:8], columns[:, 8:16]
        b1_col = columns[:, 16:32]
        lnw_col, lnb_col = columns[:, 32:33], columns[:, 33:34]
        minus_half = sbuf("minus_half", [P, ROWS])
        eps = sbuf("eps", [P, ROWS])
        slow_sb = sbuf("slow_sb", [P, H, 3 * D + 1])
        wout_sb = sbuf("wout_sb", [P, PAIRS, E])
        wg_sb = sbuf("wg_sb", [P, X])
        w1_sb = sbuf("w1_sb", [P, X, XH])
        w2_sb = sbuf("w2_sb", [P, X, NXB, E])
        b2_sb = sbuf("b2_sb", [X, E])
        late_loaded = sem("late_loaded")

        layer0(nc, sem, sbuf, locals_of(pair, flip, accum, misc, x1, ident, columns, minus_half, eps),
               x, qkv_w, qkv_b, out_w, out_b, w_gate, w_up, w_down, ln_w, ln_b, w_slow, w_out,
               Wg, W1, b1, W2, b2,
               (slow_sb, wout_sb, wg_sb, w1_sb, w2_sb, b2_sb, late_loaded))
        layer1(nc, sem, sbuf, locals_of(pair, flip, accum, misc, x1, ident, columns, minus_half, eps),
               (slow_sb, wout_sb, wg_sb, w1_sb, w2_sb, b2_sb, late_loaded), out)


def locals_of(*kept):
    return kept


def layer0(nc, sem, sbuf, kept, x, qkv_w, qkv_b, out_w, out_b, w_gate, w_up, w_down, ln_w, ln_b,
           w_slow, w_out, Wg, W1, b1, W2, b2, late):
    pair, flip, accum, misc, x1, ident, columns, minus_half, eps = kept
    slow_sb, wout_sb, wg_sb, w1_sb, w2_sb, b2_sb, late_loaded = late
    bq8, bk = columns[:, 0:8], columns[:, 8:16]
    ctx = ExitStack()
    with ctx:
        def sb(name, shape, dt=F32):
            return sbuf(name, shape, dt, ctx)

        ident_bf = sb("ident_bf", [P, P], BF16)
        mask = sb("mask", [P, P], BF16)
        stage = sb("stage", [34, P])
        outb_bc = sb("outb_bc", [P, E])
        bv_bc = sb("bv_bc", [P, H * D])
        outw_sb = sb("outw_sb", [P, PAIRS, E])
        gate_T = sb("gate_T", [P, HID])
        up_T = sb("up_T", [P, HID])
        down_T = sb("down_T", [P, HID])
        xb = sb("xb", [P, ROWS, E])
        xob = sb("xob", [P, ROWS, E])
        xn = sb("xn", [P, ROWS, E])
        xnT = sb("xnT", [P, S])
        stats = sb("stats", [P, ROWS, 6])
        mv = sb("mv", [P, ROWS, 2])
        rstd = sb("rstd", [P, ROWS])
        w_pair = sb("w_pair", [P, 3, 2, D])
        q_z = [sb("q_z0", [P, S]), sb("q_z1", [P, S])]
        k_T = sb("k_T", [P, S])
        v_sb = sb("v_sb", [P, ROWS, 2 * D])
        neg_max = sb("neg_max", [P, SCORES])
        row_sum = sb("row_sum", [P, SCORES])
        recip_x = sb("recip_x", [P, SCORES, D])
        recip_T = sb("recip_T", [P, 512])
        probs = sb("probs", [P, 2, 2, S])
        probs_T = [sb("probs_T0", [P, 2, GB, 512]), sb("probs_T1", [P, 2, ROWS, 512])]
        att_T = sb("att_T", [P, PAIRS, S])
        gate_e = probs[:, 0, 0, :]
        gate_t = probs[:, 0, 1, :]
        hid_T = probs_T[0][:, :, :, :].rearrange("p a b c -> p (a b c)")[:, 0:NHID * S] \
            .rearrange("p (j n) -> p j n", j=NHID)
        raw = att_T[:, 0:6, :].rearrange("p a b -> p (a b)").bitcast(I32)[:, 0:3 * HID] \
            .rearrange("p (w n) -> p w n", w=3)
        raw_f = probs_T[1][:, :, :, :].rearrange("p a b c -> p (a b c)")[:, 0:3 * HID] \
            .rearrange("p (w n) -> p w n", w=3)

        ints_loaded, small_loaded = sem("ints_loaded"), sem("small_loaded")
        stage_loaded, outw_loaded = sem("stage_loaded"), sem("outw_loaded")
        x_loaded, pair_loaded = sem("x_loaded"), sem("pair_loaded")
        ident_made, mask_made, const_step = sem("ident_made"), sem("mask_made"), sem("const_step")
        ints_scaled, setup_flipped, setup_copied = sem("ints_scaled"), sem("setup_flipped"), sem("setup_copied")
        bq_scaled = sem("bq_scaled")
        dve_step = sem("dve_step")
        var_ready, rstd_ready, pool_step = sem("var_ready"), sem("rstd_ready"), sem("pool_step")
        xn_ready, xn_flipped0, xn_flipped1 = sem("xn_ready"), sem("xn_flipped0"), sem("xn_flipped1")
        xnT_dve, xnT_act = sem("xnT_dve"), sem("xnT_act")
        xob_ready = sem("xob_ready")
        q_made, k_made, v_made = sem("q_made"), sem("k_made"), sem("v_made")
        q_kept, k_kept, v_kept = sem("q_kept"), sem("k_kept"), sem("v_kept")
        scores_ready, max_ready, probs_ready = sem("scores_ready"), sem("max_ready"), sem("probs_ready")
        flipped0, flipped1 = sem("flipped0"), sem("flipped1")
        flip0_kept, flip1_kept = sem("flip0_kept"), sem("flip1_kept")
        recip_ready = sem("recip_ready")
        recip_flipped, recipT_kept = sem("recip_flipped"), sem("recipT_kept")
        pv_ready, att_kept = sem("pv_ready"), sem("att_kept")
        gate_up_ready, gate_exp, hid_kept = sem("gate_up_ready"), sem("gate_exp"), sem("hid_kept")
        branch_ready, x1_kept = sem("branch_ready"), sem("x1_kept")

        x_v = x.rearrange("b (r p) e -> b p r e", p=P)
        qkv_v = qkv_w.rearrange("e (n h) (c d) -> n e c h d", h=2, c=3)
        qkvb_v = qkv_b.rearrange("(n h) (c d) -> c n h d", h=2, c=3)
        slow_v = w_slow.rearrange("e (h f) -> e h f", f=3 * D + 1)

        with nc.Block() as block:

            @block.sync
            def _(sp):
                for w, src in enumerate((w_gate, w_up)):
                    sp.dma_start(raw[:, w, :].rearrange("p (j e) -> p j e", j=NHID),
                                 src.rearrange("(j p) e -> p j e", p=P)).then_inc(ints_loaded, 16)
                sp.dma_start(raw[:, 2, :], w_down).then_inc(ints_loaded, 16)
                for c, n0 in ((0, 0), (1, PAIRS)):
                    sp.dma_start(stage[n0:n0 + PAIRS, :].rearrange("n (h d) -> n h d", h=2),
                                 qkvb_v[c]).then_inc(stage_loaded, 16)
                sp.dma_start(stage[16:32, :], b1.rearrange("x (j p) -> (x j) p", p=P)).then_inc(stage_loaded, 16)
                sp.dma_start(stage[32:33, :], ln_w.unsqueeze(0)).then_inc(stage_loaded, 16)
                sp.dma_start(stage[33:34, :], ln_b.unsqueeze(0)).then_inc(stage_loaded, 16)
                sp.dma_start(outb_bc[:], out_b.unsqueeze(0).broadcast_to([P, E])).then_inc(small_loaded, 16)
                sp.dma_start(bv_bc[:].rearrange("p (h d) -> p h d", h=H),
                             qkv_b[:, 2 * D:3 * D].unsqueeze(0).broadcast_to([P, H, D])).then_inc(small_loaded, 16)
                with sp.Fori(0, B) as b:
                    sp.wait_ge(xn_ready, b)
                    sp.wait_ge(xob_ready, b)
                    sp.dma_start(xb[:], x_v[b]).then_inc(x_loaded, 16)
                    with sp.Fori(0, PAIRS) as n:
                        sp.wait_ge(v_made, b * PAIRS + n)
                        for c in range(3):
                            sp.dma_start(w_pair[:, c, :, :], qkv_v[n, :, c]).then_inc(pair_loaded, 16)

            @block.gpsimd
            def _(pool):
                pool.memset(ident[:], 0.0).then_inc(const_step, 1)
                pool.wait_ge(const_step, 1)
                pool.affine_select(out=ident[:], in_=ident[:], compare_op=ALU.not_equal, fill=1.0, base=0,
                                   pattern=[[-1, P]], channel_multiplier=1).then_inc(ident_made, 1)
                pool.memset(minus_half[:], -0.5).then_inc(const_step, 1)
                pool.memset(mask[:], 0.0).then_inc(const_step, 1)
                pool.wait_ge(const_step, 3)
                pool.affine_select(out=mask[:], in_=mask[:], compare_op=ALU.is_ge, fill=NEG, base=0,
                                   pattern=[[-1, P]], channel_multiplier=1).then_inc(mask_made, 1)
                pool.wait_ge(ident_made, 1)
                pool.tensor_copy(ident_bf[:], ident[:]).then_inc(mask_made, 1)
                pool.wait_ge(mask_made, 2)
                pool.memset(q_z[0][D:P, :], 0.0).then_inc(mask_made, 1)
                pool.wait_ge(mask_made, 3)
                pool.memset(q_z[1][0:D, :], 0.0).then_inc(mask_made, 1)
                pool.wait_ge(mask_made, 4)
                pool.wait_ge(setup_copied, 1)
                pool.dma_start(outw_sb[:], out_w.rearrange("(n h) d e -> (h d) n e", h=2)).then_inc(outw_loaded, 16)
                pool.dma_start(slow_sb[:], slow_v).then_inc(late_loaded, 16)
                pool.dma_start(wout_sb[:], w_out.rearrange("(n p) e -> p n e", p=P)).then_inc(late_loaded, 16)
                pool.dma_start(wg_sb[:], Wg).then_inc(late_loaded, 16)
                pool.dma_start(w1_sb[:], W1.rearrange("x e h -> e x h")).then_inc(late_loaded, 16)
                pool.dma_start(w2_sb[:], W2.rearrange("x (j p) e -> p x j e", p=P)).then_inc(late_loaded, 16)
                pool.dma_start(b2_sb[:], b2).then_inc(late_loaded, 16)
                with pool.Fori(0, B) as b:
                    pool.wait_ge(var_ready, b + 1)
                    pool.tensor_tensor(rstd[:], mv[:, :, 1], eps[:], ALU.add).then_inc(pool_step, 1)
                    pool.wait_ge(pool_step, b + 1)
                    pool.tensor_tensor(rstd[:], rstd[:], minus_half[:], ALU.pow).then_inc(rstd_ready, 1)
                    pool.wait_ge(x_loaded, 16 * (b + 1))
                    pool.wait_ge(small_loaded, 32)
                    pool.wait_ge(x1_kept, 2 * b)
                    pool.tensor_tensor(xob[:], xb[:], outb_bc[:].unsqueeze(1).broadcast_to([P, ROWS, E]),
                                       ALU.add).then_inc(xob_ready, 1)

            @block.scalar
            def _(act):
                with act.Fori(0, B) as b:
                    act.wait_ge(xn_flipped1, b + 1)
                    act.activation(xnT[:, 512:1024], flip[1][:], ACT.Copy).then_inc(xnT_act, 1)
                    with act.Fori(0, PAIRS) as n:
                        it = b * PAIRS + n
                        act.wait_ge(q_made, it + 1)
                        act.wait_ge(bq_scaled, 1)
                        act.wait_ge(mask_made, 4)
                        for h in range(2):
                            r = slice(h * D, (h + 1) * D)
                            act.activation(q_z[h][r, :], pair[0][r, :], ACT.Identity, bias=bq8[r, bass.ds(n, 1)],
                                           scale=SCALE).then_inc(q_kept, 1)

                        def softmax(qb):
                            for h in range(2):
                                i = 2 * qb + h
                                act.wait_ge(max_ready, it * SCORES + i + 1)
                                L = P * (qb + 1)
                                half = 512 * (qb % 2) if qb < GB else 0
                                act.activation(probs[:, h, qb % 2, 0:L], pair[h][:, half:half + L], ACT.Exp,
                                               bias=neg_max[:, i:i + 1], accum_out=row_sum[:, i:i + 1]
                                               ).then_inc(probs_ready, 1)

                        def keep_flips(qb):
                            g = qb // GB
                            todo = [(1, 0, qb + 1)] if g == 0 else [(0, GB, qb + 1), (1, GB, qb + 1)]
                            for k, (h, lo, hi) in enumerate(todo):
                                act.wait_ge(flipped1, it * FLIPS + flips_before(qb) + k + 1)
                                at = P * (qb % GB)
                                act.activation(probs_T[g][:, h, lo:hi, at:at + P],
                                               flip[1][:, 0:P * (hi - lo)].rearrange("p (k q) -> p k q", q=P),
                                               ACT.Copy).then_inc(flip1_kept, 1)

                        def keep_recip(g):
                            act.wait_ge(recip_flipped, it * QG + g + 1)
                            act.wait_ge(att_kept, it * QG + g)
                            act.activation(recip_T[:], misc[:], ACT.Copy).then_inc(recipT_kept, 1)

                        softmax(0)
                        softmax(1)
                        for qb in range(ROWS):
                            keep_flips(qb)
                            if qb == GB - 1:
                                keep_recip(0)
                            if qb + 2 < ROWS:
                                softmax(qb + 2)
                        keep_recip(1)
                    with act.Fori(0, NHID) as j:
                        act.wait_ge(gate_up_ready, b * NHID + j + 1)
                        act.wait_ge(hid_kept, b * NHID + j)
                        act.activation(gate_e, pair[0][:], ACT.Exp, scale=-1.0).then_inc(gate_exp, 1)

            @block.vector
            def _(dve):
                dve.wait_ge(ints_loaded, 48)
                dve.tensor_scalar(raw_f, raw, INT_SCALE, None, ALU.mult).then_inc(ints_scaled, 1)
                dve.wait_ge(setup_flipped, 1)
                dve.tensor_copy(gate_T[:], pair[0][:, 0:HID]).then_inc(setup_copied, 1)
                dve.tensor_copy(up_T[:], pair[0][:, HID:2 * HID]).then_inc(setup_copied, 1)
                dve.tensor_copy(down_T[:], pair[1][:, 0:HID]).then_inc(setup_copied, 1)
                dve.tensor_copy(columns[:], pair[1][:, 512:512 + 34]).then_inc(dve_step, 1)
                dve.wait_ge(dve_step, 1)
                dve.tensor_scalar(bq8, bq8, SCALE, None, ALU.mult).then_inc(bq_scaled, 1)
                dve.wait_ge(bq_scaled, 1)
                STEPS = 1 + 3 * NHID
                with dve.Fori(0, B) as b:
                    dve.wait_ge(x_loaded, 16 * (b + 1))
                    for r in range(ROWS):
                        last = dve.bn_stats(stats[:, r, :], xb[:, r, :])
                    last.then_inc(dve_step, 1)
                    dve.wait_ge(dve_step, b * STEPS + 2)
                    dve.memset(eps[:], EPS)
                    for r in range(ROWS):
                        last = dve.bn_aggr(mv[:, r, :], stats[:, r, :])
                    last.then_inc(var_ready, 1)
                    dve.wait_ge(rstd_ready, b + 1)
                    for r in range(ROWS):
                        last = dve.tensor_scalar(xn[:, r, :], xb[:, r, :], mv[:, r, 0:1], rstd[:, r:r + 1],
                                                 ALU.subtract, ALU.mult)
                    last.then_inc(xn_ready, 1)
                    dve.wait_ge(xn_flipped0, b + 1)
                    dve.tensor_copy(xnT[:, 0:512], flip[0][:]).then_inc(xnT_dve, 1)
                    with dve.Fori(0, PAIRS) as n:
                        it = b * PAIRS + n
                        dve.wait_ge(k_made, it + 1)
                        dve.tensor_scalar(k_T[:], pair[1][:], bk[:, bass.ds(n, 1)], None, ALU.add).then_inc(k_kept, 1)
                        dve.wait_ge(v_made, it + 1)
                        dve.wait_ge(small_loaded, 32)
                        for f in range(2):
                            dve.tensor_tensor(v_sb[:, GB * f:GB * (f + 1), :],
                                              flip[f][:].rearrange("p (r d) -> p r d", r=GB),
                                              bv_bc[:, bass.ds(n * 2 * D, 2 * D)].unsqueeze(1).broadcast_to([P, GB, 2 * D]),
                                              ALU.add).then_inc(v_kept, 1)

                        def maxima(qb):
                            for h in range(2):
                                i = 2 * qb + h
                                dve.wait_ge(scores_ready, it * SCORES + i + 1)
                                L = P * (qb + 1)
                                half = 512 * (qb % 2) if qb < GB else 0
                                dve.tensor_reduce(out=neg_max[:, i:i + 1], in_=pair[h][:, half:half + L], axis=AX.X,
                                                  op=ALU.max, negate=True).then_inc(max_ready, 1)

                        def keep_flips(qb):
                            g = qb // GB
                            todo = [(0, qb + 1)] if g == 0 else [(0, GB), (1, GB)]
                            for k, (h, hi) in enumerate(todo):
                                dve.wait_ge(flipped0, it * FLIPS + flips_before(qb) + k + 1)
                                at = P * (qb % GB)
                                dve.tensor_copy(probs_T[g][:, h, 0:hi, at:at + P],
                                                flip[0][:, 0:P * hi].rearrange("p (k q) -> p k q", q=P)
                                                ).then_inc(flip0_kept, 1)

                        def invert(g):
                            dve.wait_ge(probs_ready, it * SCORES + 2 * GB * (g + 1))
                            lo = g * 2 * GB
                            dve.reciprocal(recip_x[:, lo:lo + 2 * GB, :],
                                           row_sum[:, lo:lo + 2 * GB].unsqueeze(2).broadcast_to([P, 2 * GB, D])
                                           ).then_inc(recip_ready, 1)

                        def normalise(g):
                            dve.wait_ge(recipT_kept, it * QG + g + 1)
                            dve.wait_ge(pv_ready, it * QG + g + 1)
                            dve.tensor_tensor(att_T[:, bass.ds(n, 1), 512 * g:512 * (g + 1)].rearrange("p a q -> p (a q)"),
                                              accum[:], recip_T[:], ALU.mult).then_inc(att_kept, 1)

                        maxima(0)
                        maxima(1)
                        for qb in range(ROWS):
                            keep_flips(qb)
                            if qb == GB - 1:
                                invert(0)
                            if qb + 2 < ROWS:
                                maxima(qb + 2)
                            if qb == GB - 1:
                                normalise(0)
                        invert(1)
                        normalise(1)
                    for j in range(NHID):
                        dve.wait_ge(gate_exp, b * NHID + j + 1)
                        dve.tensor_scalar(gate_t, gate_e, 1.0, None, ALU.add).then_inc(dve_step, 1)
                        dve.wait_ge(dve_step, b * STEPS + 3 * j + 3)
                        dve.reciprocal(gate_t, gate_t).then_inc(dve_step, 1)
                        dve.wait_ge(dve_step, b * STEPS + 3 * j + 4)
                        dve.tensor_tensor(gate_t, pair[0][:], gate_t, ALU.mult).then_inc(dve_step, 1)
                        dve.wait_ge(dve_step, b * STEPS + 3 * j + 5)
                        dve.tensor_tensor(hid_T[:, j, :], pair[1][:], gate_t, ALU.mult).then_inc(hid_kept, 1)
                    dve.wait_ge(xob_ready, b + 1)
                    for f in range(2):
                        dve.wait_ge(branch_ready, 2 * b + f + 1)
                        dve.tensor_tensor(x1[:, bass.ds(b, 1), GB * f:GB * (f + 1), :].rearrange("p a r e -> p (a r e)"),
                                          flip[f][:], xob[:, GB * f:GB * (f + 1), :].rearrange("p r e -> p (r e)"),
                                          ALU.add).then_inc(x1_kept, 1)

            @block.tensor
            def _(pe):
                pe.wait_ge(ident_made, 1)
                pe.wait_ge(ints_scaled, 1)
                pe.wait_ge(stage_loaded, 80)
                for w in range(2):
                    for j in range(NHID):
                        pe.transpose(pair[0][:, w * HID + j * P:w * HID + (j + 1) * P], raw_f[:, w, j * P:(j + 1) * P], ident[:])
                for j in range(NHID):
                    pe.transpose(pair[1][:, j * P:(j + 1) * P], raw_f[:, 2, j * P:(j + 1) * P], ident[:])
                pe.transpose(pair[1][:, 512:512 + 34], stage[:], ident[0:34, 0:34]).then_inc(setup_flipped, 1)
                pe.wait_ge(mask_made, 4)
                pe.wait_ge(setup_copied, 3)
                pe.wait_ge(bq_scaled, 1)
                with pe.Fori(0, B) as b:
                    pe.wait_ge(xn_ready, b + 1)
                    pe.wait_ge(x1_kept, 2 * b)
                    for r in range(ROWS):
                        last = pe.transpose(flip[r // GB][:, P * (r % GB):P * (r % GB + 1)], xn[:, r, :], ident[:])
                        if r == GB - 1:
                            last.then_inc(xn_flipped0, 1)
                    last.then_inc(xn_flipped1, 1)
                    with pe.Fori(0, PAIRS) as n:
                        it = b * PAIRS + n
                        pe.wait_ge(xnT_dve, b + 1)
                        pe.wait_ge(xnT_act, b + 1)
                        pe.wait_ge(pair_loaded, 48 * (it + 1))
                        pe.wait_ge(probs_ready, it * SCORES)
                        for c, made in ((0, q_made), (1, k_made)):
                            for half in range(2):
                                last = pe.matmul(pair[c][:, 512 * half:512 * (half + 1)],
                                                 lhsT=w_pair[:, c, :, :].rearrange("p h d -> p (h d)"),
                                                 rhs=xnT[:, 512 * half:512 * (half + 1)], start=True, stop=True)
                            last.then_inc(made, 1)
                        pe.wait_ge(flip0_kept, it * FLIPS)
                        pe.wait_ge(flip1_kept, it * FLIPS)
                        for r in range(ROWS):
                            last = pe.matmul(flip[r // GB][:, P * (r % GB):P * (r % GB + 1)],
                                             lhsT=xnT[:, P * r:P * (r + 1)],
                                             rhs=w_pair[:, 2, :, :].rearrange("p h d -> p (h d)"), start=True, stop=True)
                        last.then_inc(v_made, 1)

                        def score(qb):
                            L = P * (qb + 1)
                            for h in range(2):
                                if 2 <= qb < GB:
                                    pe.wait_ge(probs_ready, it * SCORES + 2 * (qb - 2) + h + 1)
                                elif qb >= GB:
                                    pe.wait_ge(probs_ready, it * SCORES + 2 * (qb - 1) + h + 1)
                                half = 512 * (qb % 2) if qb < GB else 0
                                for lo in range(0, L, 512):
                                    w = min(512, L - lo)
                                    diag = lo + w == L
                                    pe.matmul(pair[h][:, half + lo:half + lo + w], lhsT=q_z[h][:, P * qb:P * (qb + 1)],
                                              rhs=k_T[:, lo:lo + w], start=True, stop=not diag)
                                pe.matmul(pair[h][:, half + L - P:half + L], lhsT=ident_bf[:], rhs=mask[:],
                                          start=False, stop=True).then_inc(scores_ready, 1)

                        def flip_probs(qb):
                            at0 = flips_before(qb)
                            for h in range(2):
                                pe.wait_ge(probs_ready, it * SCORES + 2 * qb + h + 1)
                                todo = [(h, at0, 0, qb + 1)] if qb < GB else [(0, at0 + h, 0, GB), (1, at0 + h, GB, qb + 1)]
                                for f, before, lo, hi in todo:
                                    pe.wait_ge((flip0_kept, flip1_kept)[f], it * FLIPS + before)
                                    for k in range(lo, hi):
                                        last = pe.transpose(flip[f][:, P * (k - lo):P * (k - lo + 1)],
                                                            probs[:, h, qb % 2, P * k:P * (k + 1)], ident[:])
                                    last.then_inc((flipped0, flipped1)[f], 1)

                        def flip_recip(g):
                            pe.wait_ge(recip_ready, it * QG + g + 1)
                            pe.wait_ge(recipT_kept, it * QG + g)
                            for qb in range(GB):
                                i = 2 * (g * GB + qb)
                                last = pe.transpose(misc[:, P * qb:P * (qb + 1)],
                                                    recip_x[:, i:i + 2, :].rearrange("p h d -> p (h d)"), ident[:])
                            last.then_inc(recip_flipped, 1)

                        def weigh(g):
                            done = flips_before(GB * (g + 1))
                            pe.wait_ge(flip0_kept, it * FLIPS + done)
                            pe.wait_ge(flip1_kept, it * FLIPS + done)
                            pe.wait_ge(att_kept, it * QG + g)
                            keys = GB * (g + 1)
                            for k in range(keys):
                                at = P * max(0, k - GB * g)
                                for h in range(2):
                                    last = pe.matmul(accum[D * h:D * (h + 1), at:512], lhsT=v_sb[:, k, D * h:D * (h + 1)],
                                                     rhs=probs_T[g][:, h, k, at:512], start=k == 0, stop=k == keys - 1)
                            last.then_inc(pv_ready, 1)

                        pe.wait_ge(q_kept, 2 * (it + 1))
                        pe.wait_ge(k_kept, it + 1)
                        score(0)
                        score(1)
                        for qb in range(ROWS):
                            if qb == 0:
                                pe.wait_ge(v_kept, 2 * (it + 1))
                            flip_probs(qb)
                            if qb == GB - 1:
                                flip_recip(0)
                            if qb + 2 < ROWS:
                                score(qb + 2)
                            if qb == GB - 1:
                                weigh(0)
                        flip_recip(1)
                        weigh(1)
                    pe.wait_ge(probs_ready, (b + 1) * PAIRS * SCORES)
                    for j in range(NHID):
                        pe.wait_ge(hid_kept, b * NHID + j)
                        for c, w_T in enumerate((gate_T, up_T)):
                            for half in range(2):
                                last = pe.matmul(pair[c][:, 512 * half:512 * (half + 1)], lhsT=w_T[:, P * j:P * (j + 1)],
                                                 rhs=xnT[:, 512 * half:512 * (half + 1)], start=True, stop=True)
                        last.then_inc(gate_up_ready, 1)
                    pe.wait_ge(outw_loaded, 16)
                    pe.wait_ge(att_kept, (b + 1) * PAIRS * QG)
                    pe.wait_ge(hid_kept, (b + 1) * NHID)
                    for r in range(ROWS):
                        dst = flip[r // GB][:, P * (r % GB):P * (r % GB + 1)]
                        for n2 in range(PAIRS):
                            pe.matmul(dst, lhsT=att_T[:, n2, P * r:P * (r + 1)], rhs=outw_sb[:, n2, :], start=n2 == 0, stop=False)
                        for j in range(NHID):
                            last = pe.matmul(dst, lhsT=hid_T[:, j, P * r:P * (r + 1)], rhs=down_T[:, P * j:P * (j + 1)],
                                             start=False, stop=j == NHID - 1)
                        if r % GB == GB - 1:
                            last.then_inc(branch_ready, 1)


def layer1(nc, sem, sbuf, kept, late, out):
    pair, flip, accum, misc, x1, ident, columns, minus_half, eps = kept
    slow_sb, wout_sb, wg_sb, w1_sb, w2_sb, b2_sb, late_loaded = late
    b1_col, lnw_col, lnb_col = columns[:, 16:32], columns[:, 32:33], columns[:, 33:34]
    HD = H * D
    PARTS = 3 * B
    XS = X // B
    ctx = ExitStack()
    with ctx:
        def sb(name, shape, dt=F32):
            return sbuf(name, shape, dt, ctx)

        stats1 = sb("stats1", [P, B, 6])
        mv_n, mv_h = sb("mv_n", [P, B, 2]), sb("mv_h", [P, B, 2])
        rstd_n, rstd_h = sb("rstd_n", [P, B]), sb("rstd_h", [P, B])
        nrm = sb("nrm", [P, B, E])
        hat = sb("hat", [P, B, E])
        resid = sb("resid", [P, B, E])
        nrm_T = sb("nrm_T", [P, B * P])
        h_T = sb("h_T", [P, B * P])
        sig = sb("sig", [P, 2, B * H])
        beta = sb("beta", [P, B, H])
        gate = sb("gate", [P, B, X])
        stat4 = sb("stat4", [P, 4, B])
        above = sb("above", [P, B, X, X])
        equal = sb("equal", [P, B, X, X])
        earlier = sb("earlier", [P, X, X])
        rank = sb("rank", [P, B, X])
        score = sb("score", [P, B, X])
        score_T = sb("score_T", [X, B * P])
        e_buf = sb("e_buf", [P, 2, HD])
        qs = sb("qs", [P, B, HD])
        ks = sb("ks", [P, B, HD])
        vb = sb("vb", [P, B, HD])
        r_q, r_k = sb("r_q", [P, B, H]), sb("r_k", [P, B, H])
        rk_beta = sb("rk_beta", [P, B, H])
        prod = sb("prod", [P, 2 * B - 1, HD])
        coef = sb("coef", [P, 2 * B - 1, H])
        delta = sb("delta", [P, B, HD])
        part = sb("part", [P, B, HD])
        outs = sb("outs", [P, 2, HD])
        outs_T = sb("outs_T", [P, 2, PAIRS, P])
        hid = sb("hid", [P, NXB, B * P])
        moe = sb("moe", [P, B, E])
        fin = sb("fin", [P, B, E])

        earlier_step, earlier_made = sem("earlier_step"), sem("earlier_made")
        d_step, g_step = sem("d_step"), sem("g_step")
        varn_ready, rstdn_ready, varh_ready, rstdh_ready = sem("varn_ready"), sem("rstdn_ready"), sem("varh_ready"), sem("rstdh_ready")
        eps_step = sem("eps_step")
        nrm_ready, hat_ready, resid_ready = sem("nrm_ready"), sem("hat_ready"), sem("resid_ready")
        nrm_flipped, hat_flipped, nrmT_kept, hT_kept = sem("nrm_flipped"), sem("hat_flipped"), sem("nrmT_kept"), sem("hT_kept")
        small_ready, beta_low, beta_exp = sem("small_ready"), sem("beta_low"), sem("beta_exp")
        logit_ready, gate_exp = sem("logit_ready"), sem("gate_exp_l1")
        score_ready, score_flipped, scoreT_kept = sem("score_ready"), sem("score_flipped"), sem("scoreT_kept")
        part_ready, low_ready, e_ready, part_kept = sem("part_ready"), sem("low_ready"), sem("e_ready"), sem("part_kept")
        hid_ready, hid_kept = sem("hid_ready"), sem("hid_kept_l1")
        y_ready, y_kept = sem("y_ready"), sem("y_kept")
        prod_ready, prod_used = sem("prod_ready"), sem("prod_used")
        terms_ready, out_step, out_ready = sem("terms_ready"), sem("out_step"), sem("out_ready")
        out_flipped, outT_kept = sem("out_flipped"), sem("outT_kept")
        attn_ready, fin_ready, stored = sem("attn_ready"), sem("fin_ready"), sem("stored")

        out_v = out.rearrange("s (t p) e -> t p s e", p=P)

        def heads(ap):
            return ap.rearrange("p (h d) -> p h d", h=H)

        def over_heads(ap):
            return ap.unsqueeze(len(ap.shape)).broadcast_to([*ap.shape, D])

        with nc.Block() as block:

            @block.sync
            def _(sp):
                with sp.Fori(0, ROWS) as t:
                    sp.wait_ge(fin_ready, t + 1)
                    sp.dma_start(out_v[t], fin[:]).then_inc(stored, 16)
                sp.wait_ge(stored, 16 * ROWS)

            @block.gpsimd
            def _(pool):
                pool.memset(earlier[:], 1.0).then_inc(earlier_step, 1)
                pool.wait_ge(earlier_step, 1)
                pool.affine_select(out=earlier[:], in_=earlier[:], compare_op=ALU.is_gt, fill=0.0, base=0,
                                   pattern=[[1, X], [-1, X]], channel_multiplier=0).then_inc(earlier_made, 1)
                with pool.Fori(0, ROWS) as t:
                    for k, (ready, mv, rstd, done) in enumerate(((varn_ready, mv_n, rstd_n, rstdn_ready),
                                                                 (varh_ready, mv_h, rstd_h, rstdh_ready))):
                        pool.wait_ge(ready, t + 1)
                        pool.tensor_tensor(rstd[:], mv[:, :, 1], eps[:, 0:B], ALU.add).then_inc(eps_step, 1)
                        pool.wait_ge(eps_step, 2 * t + k + 1)
                        pool.tensor_tensor(rstd[:], rstd[:], minus_half[:, 0:B], ALU.pow).then_inc(done, 1)
                    pool.wait_ge(fin_ready, t)
                    pool.wait_ge(nrm_ready, t + 1)
                    pool.tensor_tensor(resid[:], nrm[:], x1[:, :, bass.ds(t, 1), :].rearrange("p s a e -> p s (a e)"),
                                       ALU.add).then_inc(resid_ready, 1)

                    def products(s):
                        pool.wait_ge(part_kept, PARTS * t + 3 * s + 2)
                        pool.wait_ge(prod_used, B * t + s)
                        if s:
                            pool.tensor_tensor(prod[:, 0:s, :], ks[:, 0:s, :],
                                               ks[:, s:s + 1, :].broadcast_to([P, s, HD]), ALU.mult).then_inc(prod_ready, 1)
                        pool.tensor_tensor(prod[:, B - 1:B + s, :], ks[:, 0:s + 1, :],
                                           qs[:, s:s + 1, :].broadcast_to([P, s + 1, HD]), ALU.mult).then_inc(prod_ready, 1)

                    def sums(s):
                        base = t * (B * (B - 1) // 2 - (B - 1)) + (s - 1) * (s - 2) // 2
                        pool.wait_ge(terms_ready, B * t + s + 1)
                        pool.wait_ge(out_flipped, B * t + max(s - 1, 0))
                        for k in range(1, s + 1):
                            if k > 1:
                                pool.wait_ge(out_step, base + k - 1)
                            first = part[:, 0, :] if k == 1 else outs[:, s % 2, :]
                            pool.tensor_tensor(outs[:, s % 2, :], first, part[:, k, :], ALU.add
                                               ).then_inc(out_ready if k == s else out_step, 1)

                    products(0)
                    products(1)
                    for s in range(2, B):
                        products(s)
                        if s > 2:
                            sums(s - 2)
                    sums(B - 2)
                    sums(B - 1)

            @block.scalar
            def _(act):
                with act.Fori(0, ROWS) as t:
                    act.wait_ge(nrm_flipped, t + 1)
                    act.activation(nrm_T[:], flip[0][:], ACT.Copy).then_inc(nrmT_kept, 1)
                    act.wait_ge(hat_flipped, t + 1)
                    act.activation(h_T[:], flip[1][:], ACT.Identity, bias=lnb_col, scale=lnw_col).then_inc(hT_kept, 1)
                    act.wait_ge(small_ready, t + 1)
                    act.activation(sig[:, 0, :], misc[:, 0:B * H], ACT.Relu, scale=-1.0).then_inc(beta_low, 1)
                    act.activation(sig[:, 1, :], misc[:, 0:B * H], ACT.Abs).then_inc(beta_low, 1)
                    act.wait_ge(beta_low, 2 * t + 2)
                    act.activation(sig[:], sig[:], ACT.Exp, scale=-1.0).then_inc(beta_exp, 1)
                    act.wait_ge(logit_ready, t + 1)
                    act.activation(gate[:], gate[:], ACT.Exp).then_inc(gate_exp, 1)

                    def exps(s):
                        for k in range(2):
                            n = 3 * s + k
                            act.wait_ge(part_ready, PARTS * t + n + 1)
                            if s:
                                act.wait_ge(part_kept, PARTS * t + n - 2)
                            act.activation(e_buf[:, k, :], pair[n % 2][:], ACT.Relu, scale=-1.0).then_inc(low_ready, 1)
                            act.wait_ge(low_ready, 2 * B * t + 2 * s + k + 1)
                            act.activation(e_buf[:, k, :], e_buf[:, k, :], ACT.Exp, scale=-1.0).then_inc(e_ready, 1)

                    def relus(e):
                        for j in range(NXB):
                            act.wait_ge(hid_ready, X * NXB * t + NXB * e + j + 1)
                            act.wait_ge(y_ready, X * t + e)
                            act.activation(hid[:, j, :], flip[j][:], ACT.Relu,
                                           bias=b1_col[:, NXB * e + j:NXB * e + j + 1]).then_inc(hid_kept, 1)

                    for s in range(B):
                        exps(s)
                        for e in range(XS * s, XS * (s + 1)):
                            relus(e)
                    act.wait_ge(score_flipped, t + 1)
                    act.activation(score_T[:], misc[0:X, :], ACT.Copy).then_inc(scoreT_kept, 1)
                    for s in range(B):
                        act.wait_ge(out_flipped, B * t + s + 1)
                        act.activation(outs_T[:, s % 2, :, :].rearrange("p n q -> p (n q)"), pair[s % 2][:], ACT.Copy
                                       ).then_inc(outT_kept, 1)

            @block.vector
            def _(dve):
                with dve.Fori(0, ROWS) as t:
                    count = [0, 0]

                    def link(op):
                        op.then_inc(d_step, 1)
                        count[0] += 1
                        dve.wait_ge(d_step, D_STEPS * t + count[0])

                    D_STEPS = 47

                    def norm(src, dst, mv, rstd, ready, rstd_ready, done):
                        for s in range(B):
                            last = dve.bn_stats(stats1[:, s, :], src(s))
                        link(last)
                        dve.memset(eps[:, 0:B], EPS)
                        for s in range(B):
                            last = dve.bn_aggr(mv[:, s, :], stats1[:, s, :])
                        last.then_inc(ready, 1)
                        dve.wait_ge(rstd_ready, t + 1)
                        for s in range(B):
                            last = dve.tensor_scalar(dst[:, s, :], src(s), mv[:, s, 0:1], rstd[:, s:s + 1],
                                                     ALU.subtract, ALU.mult)
                        last.then_inc(done, 1)

                    norm(lambda s: x1[:, s, bass.ds(t, 1), :].rearrange("p a e -> p (a e)"), nrm, mv_n, rstd_n,
                         varn_ready, rstdn_ready, nrm_ready)
                    dve.wait_ge(nrm_ready, t + 1)
                    norm(lambda s: nrm[:, s, :], hat, mv_h, rstd_h, varh_ready, rstdh_ready, hat_ready)

                    dve.wait_ge(beta_exp, t + 1)
                    link(dve.tensor_scalar(sig[:, 1, :], sig[:, 1, :], 1.0, None, ALU.add))
                    link(dve.reciprocal(sig[:, 1, :], sig[:, 1, :]))
                    link(dve.tensor_tensor(beta[:].rearrange("p s h -> p (s h)"), sig[:, 0, :], sig[:, 1, :], ALU.mult))

                    mx, total, top_sum, inv = (stat4[:, k, :] for k in range(4))

                    def over(ap):
                        return ap.unsqueeze(2).broadcast_to([P, B, X])

                    logits = misc[:, B * H:B * (H + X)].rearrange("p (s x) -> p s x", s=B)
                    dve.wait_ge(small_ready, t + 1)
                    link(dve.tensor_reduce(out=mx, in_=logits, axis=AX.X, op=ALU.max))
                    dve.tensor_tensor(gate[:], logits, over(mx), ALU.subtract).then_inc(logit_ready, 1)
                    dve.wait_ge(gate_exp, t + 1)
                    link(dve.tensor_reduce(out=total, in_=gate[:], axis=AX.X, op=ALU.add))
                    link(dve.reciprocal(inv, total))
                    link(dve.tensor_tensor(gate[:], gate[:], over(inv), ALU.mult))
                    mine = gate[:].unsqueeze(3).broadcast_to([P, B, X, X])
                    other = gate[:].unsqueeze(2).broadcast_to([P, B, X, X])
                    dve.tensor_tensor(above[:], other, mine, ALU.is_gt)
                    link(dve.tensor_tensor(equal[:], other, mine, ALU.is_equal))
                    dve.wait_ge(earlier_made, 1)
                    link(dve.tensor_tensor(equal[:], equal[:], earlier[:].unsqueeze(1).broadcast_to([P, B, X, X]), ALU.mult))
                    link(dve.tensor_tensor(above[:], above[:], equal[:], ALU.add))
                    link(dve.tensor_reduce(out=rank[:], in_=above[:], axis=AX.X, op=ALU.add))
                    link(dve.scalar_tensor_tensor(rank[:], rank[:], float(TOP), gate[:], ALU.is_lt, ALU.mult))
                    link(dve.tensor_reduce(out=top_sum, in_=rank[:], axis=AX.X, op=ALU.add))
                    link(dve.reciprocal(inv, top_sum))
                    dve.tensor_tensor(score[:], rank[:], over(inv), ALU.mult).then_inc(score_ready, 1)
                    dve.wait_ge(score_ready, t + 1)

                    def keep(s):
                        for k, dst in ((0, qs), (1, ks)):
                            dve.wait_ge(e_ready, 2 * B * t + 2 * s + k + 1)
                            n = 3 * s + k
                            dve.scalar_tensor_tensor(dst[:, s, :], pair[n % 2][:], 0.0, e_buf[:, k, :],
                                                     ALU.max, ALU.add).then_inc(part_kept, 1)
                        n = 3 * s + 2
                        dve.wait_ge(part_ready, PARTS * t + n + 1)
                        dve.tensor_tensor(heads(vb[:, s, :]), heads(pair[n % 2][:]), over_heads(beta[:, s, :]),
                                          ALU.mult).then_inc(part_kept, 1)
                        dve.wait_ge(part_kept, PARTS * t + 3 * s + 2)
                        dve.tensor_reduce(out=r_q[:, s, :], in_=heads(qs[:, s, :]), axis=AX.X, op=ALU.add)
                        link(dve.tensor_reduce(out=r_k[:, s, :], in_=heads(ks[:, s, :]), axis=AX.X, op=ALU.add))
                        dve.reciprocal(r_q[:, s, :], r_q[:, s, :])
                        link(dve.reciprocal(r_k[:, s, :], r_k[:, s, :]))
                        link(dve.tensor_tensor(rk_beta[:, s, :], r_k[:, s, :], beta[:, s, :], ALU.mult))

                    def gather(e):
                        dve.wait_ge(y_ready, X * t + e + 1)
                        for s in range(B):
                            src = accum[:, P * s:P * (s + 1)]
                            if e == 0:
                                last = dve.tensor_scalar(moe[:, s, :], src, score[:, s, e:e + 1], None, ALU.mult)
                            else:
                                last = dve.scalar_tensor_tensor(moe[:, s, :], src, score[:, s, e:e + 1], moe[:, s, :],
                                                                ALU.mult, ALU.add)
                        last.then_inc(y_kept, 1)

                    def scan(s):
                        dve.wait_ge(prod_ready, (2 * B - 1) * t + 2 * s + 1)
                        dve.wait_ge(terms_ready, B * t + s)
                        if s:
                            dve.tensor_reduce(out=coef[:, 0:s, :], in_=prod[:, 0:s, :].rearrange("p s (h d) -> p s h d", h=H),
                                              axis=AX.X, op=ALU.add)
                        red = dve.tensor_reduce(out=coef[:, B - 1:B + s, :],
                                                in_=prod[:, B - 1:B + s, :].rearrange("p s (h d) -> p s h d", h=H),
                                                axis=AX.X, op=ALU.add)
                        red.then_inc(prod_used, 1)
                        dve.wait_ge(prod_used, B * t + s + 1)
                        if s:
                            dve.tensor_tensor(coef[:, 0:s, :], coef[:, 0:s, :], r_k[:, 0:s, :], ALU.mult)
                        link(dve.tensor_tensor(coef[:, B - 1:B + s, :], coef[:, B - 1:B + s, :], r_k[:, 0:s + 1, :], ALU.mult))
                        if s:
                            dve.tensor_tensor(coef[:, 0:s, :], coef[:, 0:s, :],
                                              rk_beta[:, s:s + 1, :].broadcast_to([P, s, H]), ALU.mult)
                        link(dve.tensor_tensor(coef[:, B - 1:B + s, :], coef[:, B - 1:B + s, :],
                                               r_q[:, s:s + 1, :].broadcast_to([P, s + 1, H]), ALU.mult))
                        if s:
                            if s > 1:
                                dve.wait_ge(out_ready, (B - 1) * t + s - 1)
                            link(dve.tensor_tensor(part[:, 0:s, :].rearrange("p s (h d) -> p (s h) d", h=H),
                                                   delta[:, 0:s, :].rearrange("p s (h d) -> p (s h) d", h=H),
                                                   over_heads(coef[:, 0:s, :].rearrange("p s h -> p (s h)")), ALU.mult))
                            for k in range(s):
                                first = vb[:, s, :] if k == 0 else delta[:, s, :]
                                link(dve.tensor_tensor(delta[:, s, :], first, part[:, k, :], ALU.subtract))
                        else:
                            link(dve.tensor_copy(delta[:, 0, :], vb[:, 0, :]))
                        dst = part[:, 0:s + 1, :].rearrange("p s (h d) -> p (s h) d", h=H)
                        if s == 0:
                            dst = heads(outs[:, 0, :])
                        dve.tensor_tensor(dst, delta[:, 0:s + 1, :].rearrange("p s (h d) -> p (s h) d", h=H),
                                          over_heads(coef[:, B - 1:B + s, :].rearrange("p s h -> p (s h)")), ALU.mult
                                          ).then_inc(terms_ready, 1)

                    for s in range(2):
                        keep(s)
                        for e in range(XS * s, XS * (s + 1)):
                            gather(e)
                    scan(0)
                    for s in range(2, B):
                        keep(s)
                        for e in range(XS * s, XS * (s + 1)):
                            gather(e)
                        scan(s - 1)
                    scan(B - 1)

                    dve.wait_ge(y_kept, X * (t + 1))
                    dve.wait_ge(attn_ready, t + 1)
                    dve.wait_ge(stored, 16 * t)
                    link(dve.tensor_tensor(fin[:].rearrange("p s e -> p (s e)"), accum[:], moe[:].rearrange("p s e -> p (s e)"), ALU.add))
                    dve.wait_ge(resid_ready, t + 1)
                    dve.tensor_tensor(fin[:], fin[:], resid[:], ALU.add).then_inc(fin_ready, 1)
                    assert count[0] == D_STEPS, count

            @block.tensor
            def _(pe):
                pe.wait_ge(late_loaded, 16 * 6)
                with pe.Fori(0, ROWS) as t:
                    pe.wait_ge(nrm_ready, t + 1)
                    pe.wait_ge(hid_kept, X * NXB * t)
                    for s in range(B):
                        last = pe.transpose(flip[0][:, P * s:P * (s + 1)], nrm[:, s, :], ident[:])
                    last.then_inc(nrm_flipped, 1)
                    pe.wait_ge(hat_ready, t + 1)
                    for s in range(B):
                        last = pe.transpose(flip[1][:, P * s:P * (s + 1)], hat[:, s, :], ident[:])
                    last.then_inc(hat_flipped, 1)
                    pe.wait_ge(nrmT_kept, t + 1)
                    pe.wait_ge(hT_kept, t + 1)
                    pe.wait_ge(scoreT_kept, t)
                    for s in range(B):
                        rows = slice(P * s, P * (s + 1))
                        pe.matmul(misc[:, H * s:H * (s + 1)], lhsT=h_T[:, rows], rhs=slow_sb[:, :, 3 * D], start=True, stop=True)
                    for s in range(B):
                        rows = slice(P * s, P * (s + 1))
                        last = pe.matmul(misc[:, B * H + X * s:B * H + X * (s + 1)], lhsT=nrm_T[:, rows], rhs=wg_sb[:],
                                         start=True, stop=True)
                    last.then_inc(small_ready, 1)

                    def project(s):
                        for c in range(3):
                            n = 3 * s + c
                            if n >= 2:
                                pe.wait_ge(part_kept, PARTS * t + n - 1)
                            else:
                                pe.wait_ge(outT_kept, B * t)
                            for half in range(2):
                                last = pe.matmul(pair[n % 2][:, 512 * half:512 * (half + 1)], lhsT=h_T[:, P * s:P * (s + 1)],
                                                 rhs=slow_sb[:, 8 * half:8 * (half + 1), c * D:(c + 1) * D],
                                                 start=True, stop=True)
                            last.then_inc(part_ready, 1)

                    def expert(e):
                        for j in range(NXB):
                            pe.wait_ge(hid_kept, X * NXB * t + max(NXB * (e - 1) + j + 1, 0))
                            pe.matmul(flip[j][:], lhsT=w1_sb[:, e, P * j:P * (j + 1)], rhs=nrm_T[:], start=True,
                                      stop=True).then_inc(hid_ready, 1)
                        pe.wait_ge(hid_kept, X * NXB * t + NXB * (e + 1))
                        if e:
                            pe.wait_ge(y_kept, X * t + e)
                        else:
                            pe.wait_ge(fin_ready, t)
                        for s in range(B):
                            for j in range(NXB):
                                last = pe.matmul(accum[:, P * s:P * (s + 1)], lhsT=hid[:, j, P * s:P * (s + 1)],
                                                 rhs=w2_sb[:, e, j, :], start=j == 0, stop=j == NXB - 1)
                        last.then_inc(y_ready, 1)

                    for s in range(B):
                        project(s)
                        for e in range(XS * s, XS * (s + 1)):
                            expert(e)

                    pe.wait_ge(score_ready, t + 1)
                    for s in range(B):
                        last = pe.transpose(misc[0:X, P * s:P * (s + 1)], score[:, s, :], ident[:])
                    last.then_inc(score_flipped, 1)

                    def flip_out(s):
                        if s == 0:
                            pe.wait_ge(terms_ready, B * t + 1)
                        else:
                            pe.wait_ge(out_ready, (B - 1) * t + s)
                        if s >= 2:
                            pe.wait_ge(outT_kept, B * t + s - 1)
                        else:
                            pe.wait_ge(part_kept, PARTS * (t + 1))
                        for n in range(PAIRS):
                            last = pe.transpose(pair[s % 2][:, P * n:P * (n + 1)], outs[:, s % 2, P * n:P * (n + 1)], ident[:])
                        last.then_inc(out_flipped, 1)

                    def join(s):
                        pe.wait_ge(outT_kept, B * t + s + 1)
                        if s == 0:
                            pe.wait_ge(scoreT_kept, t + 1)
                            pe.wait_ge(y_kept, X * (t + 1))
                        dst = accum[:, P * s:P * (s + 1)]
                        pe.matmul(dst, lhsT=score_T[:, P * s:P * (s + 1)], rhs=b2_sb[:], start=True, stop=False)
                        for n in range(PAIRS):
                            last = pe.matmul(dst, lhsT=outs_T[:, s % 2, n, :], rhs=wout_sb[:, n, :], start=False, stop=n == PAIRS - 1)
                        if s == B - 1:
                            last.then_inc(attn_ready, 1)

                    flip_out(0)
                    for s in range(1, B):
                        flip_out(s)
                        join(s - 1)
                    join(B - 1)


_INS = ['L0_attn_x', 'L0_attn_qkv_w', 'L0_attn_qkv_b', 'L0_attn_out_w', 'L0_attn_out_b', 'L0_ffn_w_gate', 'L0_ffn_w_up',
        'L0_ffn_w_down', 'L1_attn_ln_w', 'L1_attn_ln_b', 'L1_attn_w_slow', 'L1_attn_w_out', 'L1_ffn_Wg', 'L1_ffn_W1',
        'L1_ffn_b1', 'L1_ffn_W2', 'L1_ffn_b2']


def kernel(**inputs):
    import numpy as np
    import concourse.bacc as bacc
    from concourse.bass_utils import run_bass_kernel_spmd

    nc = bacc.Bacc("TRN2", target_bir_lowering=False, num_devices=1)
    arrays, args = {}, []
    for name in _INS:
        a = np.ascontiguousarray(inputs[name])
        arrays[f"in_{name}"] = a
        args.append(nc.dram_tensor(f"in_{name}", a.shape, mybir.dt.from_np(a.dtype), kind="ExternalInput").ap())
    out = nc.dram_tensor("out_0", (B, S, E), F32, kind="ExternalOutput").ap()
    block_kernel(nc, *args, out)
    r = run_bass_kernel_spmd(nc, [arrays], core_ids=[0])
    return r.results[0]["out_0"]
```

```python
from contextlib import ExitStack

import concourse.bass as bass
from concourse import mybir

F32 = mybir.dt.float32
F32R = mybir.dt.float32r
BF16 = mybir.dt.bfloat16
I32 = mybir.dt.int32
ALU = mybir.AluOpType
ACT = mybir.ActivationFunctionType
AX = mybir.AxisListType

P = 128
E = 128
B, S = 4, 1024
ROWS = S // P
H, D = 16, 64
PAIRS = H // 2
HID = 384
NHID = HID // P
X, XH, NXB = 8, 256, 2
TOP = 2
QG = 2
GB = ROWS // QG
EPS = 1e-5
SCALE = D ** -0.5
INT_SCALE = 1.0 / 127.0
MASKED = -0.7 * 3.4028234663852886e38
COLUMNS = 2 * H + X * NXB + 2
CREDIT = 1

SCORES = 2 * ROWS
FLIPS = GB + 2 * GB


def flips_before(qb):
    return qb if qb < GB else GB + 2 * (qb - GB)


def block_kernel(nc, x, qkv_w, qkv_b, out_w, out_b, w_gate, w_up, w_down, ln_w, ln_b, w_slow, w_out,
                 Wg, W1, b1, W2, b2, out):
    top = ExitStack()
    with top:
        def sem(name):
            return top.enter_context(nc.semaphore(name))

        def sbuf(name, shape, dt=F32, where=top):
            return where.enter_context(nc.sbuf_tensor(name, shape, dt))

        def psum(name, shape, dt=F32):
            return top.enter_context(nc.psum_tensor(name, shape, dt))

        pair = [psum("pair0", [P, 1024]), psum("pair1", [P, 1024])]
        flip = [psum("flip0", [P, 512]), psum("flip1", [P, 512])]
        accum = psum("accum", [P, 512])
        misc = psum("misc", [P, 512])

        x1 = sbuf("x1", [P, B, ROWS, E])
        ident = sbuf("ident", [P, P])
        columns = sbuf("columns", [P, COLUMNS])
        minus_half = sbuf("minus_half", [P, ROWS])
        eps = sbuf("eps", [P, ROWS])
        slow_sb = sbuf("slow_sb", [P, H, 3 * D + 1])
        wout_sb = sbuf("wout_sb", [P, PAIRS, E])
        wg_sb = sbuf("wg_sb", [P, X])
        b2_sb = sbuf("b2_sb", [X, E])
        late_loaded = sem("late_loaded")

        kept = pair, flip, accum, misc, x1, ident, columns, minus_half, eps
        late = slow_sb, wout_sb, wg_sb, b2_sb, late_loaded
        layer0(nc, sem, sbuf, kept, x, qkv_w, qkv_b, out_w, out_b, w_gate, w_up, w_down, ln_w, ln_b,
               w_slow, w_out, Wg, b1, b2, late)
        layer1(nc, sem, sbuf, kept, W1, W2, late, out)


def layer0(nc, sem, sbuf, kept, x, qkv_w, qkv_b, out_w, out_b, w_gate, w_up, w_down, ln_w, ln_b, w_slow, w_out, Wg, b1, b2, late):
    pair, flip, accum, misc, x1, ident, columns, minus_half, eps = kept
    slow_sb, wout_sb, wg_sb, b2_sb, late_loaded = late
    bq8, bk = columns[:, 0:H], columns[:, H:2 * H]
    ctx = ExitStack()
    with ctx:
        def sb(name, shape, dt=F32):
            return sbuf(name, shape, dt, ctx)

        ident_bf = sb("ident_bf", [P, P], BF16)
        mask = sb("mask", [P, P], BF16)
        stage = sb("stage", [COLUMNS, P])
        outb_bc = sb("outb_bc", [P, E])
        bv_bc = sb("bv_bc", [P, H * D])
        outw_sb = sb("outw_sb", [P, PAIRS, E])
        gate_T = sb("gate_T", [P, HID])
        up_T = sb("up_T", [P, HID])
        down_T = sb("down_T", [P, HID])
        xn_all = sb("xn_all", [P, B, ROWS, E])
        xn = sb("xn", [P, ROWS, E])
        xnT = sb("xnT", [P, S])
        stats = sb("stats", [P, ROWS, 6])
        mv = sb("mv", [P, ROWS, 2])
        rstd = sb("rstd", [P, ROWS])
        w_qk = sb("w_qk", [P, 2, 2, 2, D])
        w_v = sb("w_v", [P, 2, D])
        q_st = [sb(f"q_st{h}", [P, S], F32R) for h in range(2)]
        k_hi = [sb(f"k_hi{h}", [P, S], F32R) for h in range(2)]
        k_lo = [sb(f"k_lo{h}", [P, S], F32R) for h in range(2)]
        v_sb = sb("v_sb", [P, ROWS, 2 * D])
        neg_max = sb("neg_max", [P, SCORES])
        row_sum = sb("row_sum", [P, SCORES])
        recip = sb("recip", [P, 2 * GB])
        recip_x = sb("recip_x", [P, 2 * GB, D])
        recip_T = sb("recip_T", [P, 512])
        probs = sb("probs", [P, 2, 2, S])
        probs_T = sb("probs_T", [P, 2, ROWS, 512])
        att_T = sb("att_T", [P, PAIRS, S])
        act_gate = sb("act_gate", [P, S])
        hid_T = sb("hid_T", [P, NHID, S])
        raw = att_T[:, 0:2, :].rearrange("p a b -> p (a b)").bitcast(I32)[:, 0:3 * HID] \
            .rearrange("p (w n) -> p w n", w=3)
        raw_f = hid_T[:, 0:2, :].rearrange("p a b -> p (a b)")[:, 0:3 * HID].rearrange("p (w n) -> p w n", w=3)

        zero = sb("zero", [P, E])
        scale_row = sb("scale_row", [P, 4 * D])
        consts_made = sem("consts_made")
        ints_loaded, small_loaded = sem("ints_loaded"), sem("small_loaded")
        stage_loaded, outw_loaded = sem("stage_loaded"), sem("outw_loaded")
        x_loaded, pair_loaded, q_scaled = sem("x_loaded"), sem("pair_loaded"), sem("q_scaled")
        ident_made, mask_made, const_step = sem("ident_made"), sem("mask_made"), sem("const_step")
        ints_scaled, setup_flipped, setup_copied = sem("ints_scaled"), sem("setup_flipped"), sem("setup_copied")
        bq_scaled, dve_step = sem("bq_scaled"), sem("dve_step")
        var_ready, rstd_ready, pool_step = sem("var_ready"), sem("rstd_ready"), sem("pool_step")
        xn_ready, xob_ready, xn_placed = sem("xn_ready"), sem("xob_ready"), sem("xn_placed")
        xn_flipped0, xn_flipped1 = sem("xn_flipped0"), sem("xn_flipped1")
        xnT_dve, xnT_act = sem("xnT_dve"), sem("xnT_act")
        proj_made, hi_kept, lo_kept = sem("proj_made"), sem("hi_kept"), sem("lo_kept")
        v_made, v_kept = sem("v_made"), sem("v_kept")
        scores_ready, max_ready, probs_ready = sem("scores_ready"), sem("max_ready"), sem("probs_ready")
        flipped0, flipped1 = sem("flipped0"), sem("flipped1")
        flip0_kept, flip1_kept = sem("flip0_kept"), sem("flip1_kept")
        recip_step, recip_ready = sem("recip_step"), sem("recip_ready")
        recip_flipped, recipT_kept = sem("recip_flipped"), sem("recipT_kept")
        pv_ready, att_kept = sem("pv_ready"), sem("att_kept")
        gate_ready, up_ready, silu_ready, hid_kept = sem("gate_ready"), sem("up_ready"), sem("silu_ready"), sem("hid_kept")
        branch_ready, x1_kept = sem("branch_ready"), sem("x1_kept")

        x_v = x.rearrange("b (r p) e -> b p r e", p=P)
        qkv_v = qkv_w.rearrange("e (n h) (c d) -> n e c h d", h=2, c=3)
        qkvb_v = qkv_b.rearrange("h (c d) -> c h d", c=3)

        def group(qb):
            return qb // GB, (GB if qb < GB else 0)

        def columns_of(qb):
            half = 512 * (qb % 2) if qb < GB else 0
            return slice(half, half + P * (qb + 1))

        with nc.Block() as block:

            @block.sync
            def _(sp):
                with sp.Fori(0, B) as b:
                    sp.dma_start(x1[:, bass.ds(b, 1), :, :].rearrange("p a r e -> p (a r) e"), x_v[b]).then_inc(x_loaded, 16)
                for w, src in enumerate((w_gate, w_up)):
                    sp.dma_start(raw[:, w, :].rearrange("p (j e) -> p j e", j=NHID),
                                 src.rearrange("(j p) e -> p j e", p=P)).then_inc(ints_loaded, 16)
                sp.dma_start(raw[:, 2, :], w_down).then_inc(ints_loaded, 16)
                for c in range(2):
                    for copy in range(2):
                        sp.dma_start(stage[c * H:(c + 1) * H, copy * D:(copy + 1) * D], qkvb_v[c]).then_inc(stage_loaded, 16)
                sp.dma_start(stage[2 * H:2 * H + X * NXB, :], b1.rearrange("x (j p) -> (x j) p", p=P)).then_inc(stage_loaded, 16)
                sp.dma_start(stage[COLUMNS - 2:COLUMNS - 1, :], ln_w.unsqueeze(0)).then_inc(stage_loaded, 16)
                sp.dma_start(stage[COLUMNS - 1:COLUMNS, :], ln_b.unsqueeze(0)).then_inc(stage_loaded, 16)
                sp.dma_start(outb_bc[:], out_b.unsqueeze(0).broadcast_to([P, E])).then_inc(small_loaded, 16)
                sp.dma_start(bv_bc[:].rearrange("p (h d) -> p h d", h=H),
                             qkv_b[:, 2 * D:3 * D].unsqueeze(0).broadcast_to([P, H, D])).then_inc(small_loaded, 16)
                with sp.Fori(0, B) as b:
                    with sp.Fori(0, PAIRS) as n:
                        sp.wait_ge(v_made, b * PAIRS + n + CREDIT)
                        for c in range(2):
                            for copy in range(2):
                                sp.dma_start(w_qk[:, c, :, copy, :], qkv_v[n, :, c]).then_inc(pair_loaded, 16)
                        sp.dma_start(w_v[:], qkv_v[n, :, 2]).then_inc(pair_loaded, 16)

            @block.gpsimd
            def _(pool):
                pool.memset(ident[:], 0.0).then_inc(const_step, 1)
                pool.wait_ge(const_step, 1)
                pool.affine_select(out=ident[:], in_=ident[:], compare_op=ALU.not_equal, fill=1.0, base=0,
                                   pattern=[[-1, P]], channel_multiplier=1).then_inc(ident_made, 1)
                pool.memset(minus_half[:], -0.5).then_inc(const_step, 1)
                pool.memset(mask[:], 0.0).then_inc(const_step, 1)
                pool.wait_ge(const_step, 3)
                pool.affine_select(out=mask[:], in_=mask[:], compare_op=ALU.is_ge, fill=MASKED, base=0,
                                   pattern=[[-1, P]], channel_multiplier=1).then_inc(mask_made, 1)
                pool.wait_ge(ident_made, 1)
                pool.tensor_copy(ident_bf[:], ident[:]).then_inc(mask_made, 1)
                with pool.Fori(0, B) as b:
                    pool.wait_ge(var_ready, b + 1)
                    pool.tensor_tensor(rstd[:], mv[:, :, 1], eps[:], ALU.add).then_inc(pool_step, 1)
                    pool.wait_ge(pool_step, b + 1)
                    pool.tensor_tensor(rstd[:], rstd[:], minus_half[:], ALU.pow).then_inc(rstd_ready, 1)
                pool.wait_ge(ints_scaled, 1)
                pool.dma_start(outw_sb[:], out_w.rearrange("(n h) d e -> (h d) n e", h=2)).then_inc(outw_loaded, 16)
                pool.dma_start(slow_sb[:], w_slow.rearrange("e (h f) -> e h f", h=H)).then_inc(late_loaded, 16)
                pool.dma_start(wout_sb[:], w_out.rearrange("(n p) e -> p n e", p=P)).then_inc(late_loaded, 16)
                pool.dma_start(wg_sb[:], Wg).then_inc(late_loaded, 16)
                pool.dma_start(b2_sb[:], b2).then_inc(late_loaded, 16)
                with pool.Fori(0, B) as b:
                    pool.wait_ge(xn_ready, b + 1)
                    pool.wait_ge(xn_flipped1, b + CREDIT)
                    pool.wait_ge(consts_made, 2)
                    pool.tensor_tensor(xn[:], xn_all[:, bass.ds(b, 1), :, :].rearrange("p a r e -> p (a r) e"),
                                       zero[:].unsqueeze(1).broadcast_to([P, ROWS, E]), ALU.add).then_inc(xn_placed, 1)
                    pool.wait_ge(small_loaded, 32)
                    pool.tensor_tensor(x1[:, bass.ds(b, 1), :, :].rearrange("p a r e -> p (a r) e"),
                                       x1[:, bass.ds(b, 1), :, :].rearrange("p a r e -> p (a r) e"),
                                       outb_bc[:].unsqueeze(1).broadcast_to([P, ROWS, E]), ALU.add).then_inc(xob_ready, 1)
                    with pool.Fori(0, PAIRS) as n:
                        pool.wait_ge(pair_loaded, 80 * (b * PAIRS + n + 1))
                        pool.tensor_tensor(w_qk[:, 0, :, :, :].rearrange("p h c d -> p (h c d)"),
                                           w_qk[:, 0, :, :, :].rearrange("p h c d -> p (h c d)"),
                                           scale_row[:], ALU.mult).then_inc(q_scaled, 1)

            @block.scalar
            def _(act):
                act.sem_inc(probs_ready, CREDIT)
                act.sem_inc(flip1_kept, CREDIT)
                act.sem_inc(recipT_kept, CREDIT)

                def keep_part(it, n, h, c):
                    act.wait_ge(proj_made, 4 * it + 2 * c + h + 1)
                    act.wait_ge(bq_scaled, 1)
                    bias = (bq8, bk)[c]
                    act.activation((q_st, k_hi)[c][h][:], pair[h][:], ACT.Identity, bias=bias[:, bass.ds(2 * n + h, 1)]
                                   ).then_inc(hi_kept, 1)

                def softmax(it, qb, h):
                    i = 2 * qb + h
                    act.wait_ge(max_ready, it * SCORES + i + 1)
                    act.activation(probs[:, h, qb % 2, 0:P * (qb + 1)], pair[h][:, columns_of(qb)], ACT.Exp,
                                   bias=neg_max[:, i:i + 1], accum_out=row_sum[:, i:i + 1]).then_inc(probs_ready, 1)

                def keep_flip(it, qb, h):
                    g, key0 = group(qb)
                    lo = 0 if g == 0 else GB
                    act.wait_ge(flipped1, it * FLIPS + flips_before(qb) + (h if g else 0) + 1)
                    at = P * (qb % GB)
                    act.activation(probs_T[:, h, key0 + lo:key0 + qb + 1, at:at + P],
                                   flip[1][:, 0:P * (qb + 1 - lo)].rearrange("p (k q) -> p k q", q=P),
                                   ACT.Copy).then_inc(flip1_kept, 1)

                def keep_recip(it, g):
                    act.wait_ge(recip_flipped, it * QG + g + 1 + CREDIT)
                    act.wait_ge(att_kept, it * QG + g + CREDIT)
                    act.activation(recip_T[:], misc[:], ACT.Copy).then_inc(recipT_kept, 1)

                def begin(it):
                    for qb in range(2):
                        for h in range(2):
                            softmax(it, qb, h)

                def unit(it, n, more):
                    for qb in range(2):
                        keep_flip(it, qb, 1)
                        for h in range(2):
                            softmax(it, qb + 2, h)
                    keep_flip(it, 2, 1)
                    for h in range(2):
                        softmax(it, 4, h)
                    keep_flip(it, 3, 1)
                    softmax(it, 5, 0)
                    keep_recip(it, 0)
                    keep_flip(it, 4, 0)
                    softmax(it, 5, 1)
                    keep_flip(it, 4, 1)
                    for qb in range(5, ROWS - 1):
                        for h in range(2):
                            softmax(it, qb + 1, h)
                            keep_flip(it, qb, h)
                    for h in range(2):
                        if more:
                            keep_part(it + 1, n + 1, h, 0)
                        keep_flip(it, ROWS - 1, h)
                    if more:
                        keep_part(it + 1, n + 1, 0, 1)
                    keep_recip(it, 1)
                    if more:
                        keep_part(it + 1, n + 1, 1, 1)
                        begin(it + 1)

                with act.Fori(0, B) as b:
                    act.wait_ge(xn_flipped1, b + 1 + CREDIT)
                    act.activation(xnT[:, 512:1024], flip[1][:], ACT.Copy).then_inc(xnT_act, 1)
                    for c in range(2):
                        for h in range(2):
                            keep_part(b * PAIRS, 0, h, c)
                    for j in range(NHID):
                        act.wait_ge(gate_ready, b * NHID + j + 1)
                        act.wait_ge(hid_kept, b * NHID + j + CREDIT)
                        act.activation(act_gate[:], pair[0][:], ACT.Silu).then_inc(silu_ready, 1)
                    begin(b * PAIRS)
                    with act.Fori(0, PAIRS - 1) as n:
                        unit(b * PAIRS + n, n, True)
                    unit(b * PAIRS + PAIRS - 1, PAIRS - 1, False)

            @block.vector
            def _(dve):
                dve.sem_inc(flip0_kept, CREDIT)
                dve.sem_inc(att_kept, CREDIT)
                dve.sem_inc(hid_kept, CREDIT)
                dve.sem_inc(x1_kept, CREDIT)
                dve.memset(zero[:], 0.0).then_inc(consts_made, 1)
                dve.memset(scale_row[:], SCALE).then_inc(consts_made, 1)
                with dve.Fori(0, B) as b:
                    dve.wait_ge(x_loaded, 16 * B)
                    rows = [x1[:, bass.ds(b, 1), r, :].rearrange("p a e -> p (a e)") for r in range(ROWS)]
                    for r in range(ROWS):
                        last = dve.bn_stats(stats[:, r, :], rows[r])
                    last.then_inc(dve_step, 1)
                    dve.wait_ge(dve_step, b + 1)
                    dve.memset(eps[:], EPS)
                    for r in range(ROWS):
                        last = dve.bn_aggr(mv[:, r, :], stats[:, r, :])
                    last.then_inc(var_ready, 1)
                    dve.wait_ge(rstd_ready, b + 1)
                    for r in range(ROWS):
                        last = dve.tensor_scalar(xn_all[:, bass.ds(b, 1), r, :].rearrange("p a e -> p (a e)"), rows[r],
                                                 mv[:, r, 0:1], rstd[:, r:r + 1], ALU.subtract, ALU.mult)
                    last.then_inc(xn_ready, 1)
                dve.wait_ge(ints_loaded, 48)
                dve.tensor_scalar(raw_f, raw, INT_SCALE, None, ALU.mult).then_inc(ints_scaled, 1)
                dve.wait_ge(setup_flipped, 1)
                dve.tensor_copy(gate_T[:], pair[0][:, 0:HID]).then_inc(setup_copied, 1)
                dve.tensor_copy(up_T[:], pair[0][:, HID:2 * HID]).then_inc(setup_copied, 1)
                dve.tensor_copy(down_T[:], pair[1][:, 0:HID]).then_inc(setup_copied, 1)
                dve.tensor_copy(columns[:], pair[1][:, 512:512 + COLUMNS]).then_inc(setup_copied, 1)
                dve.wait_ge(setup_copied, 4)
                dve.tensor_scalar(bq8, bq8, SCALE, None, ALU.mult).then_inc(bq_scaled, 1)
                dve.wait_ge(bq_scaled, 1)
                dve.wait_ge(small_loaded, 32)

                def keep_rest(it, n, h, c):
                    dve.wait_ge(hi_kept, 4 * it + 2 * c + h + 1)
                    rows = slice(D, P) if c == 0 else slice(0, P)
                    bias = (bq8, bk)[c]
                    dve.scalar_tensor_tensor((q_st, k_lo)[c][h][rows, :], pair[h][rows, :], bias[rows, bass.ds(2 * n + h, 1)],
                                             (q_st, k_hi)[c][h][rows, :].bitcast(F32), ALU.add, ALU.subtract
                                             ).then_inc(lo_kept, 1)

                def maximum(it, qb, h):
                    i = 2 * qb + h
                    dve.wait_ge(scores_ready, it * SCORES + i + 1)
                    dve.tensor_reduce(out=neg_max[:, i:i + 1], in_=pair[h][:, columns_of(qb)], axis=AX.X,
                                      op=ALU.max, negate=True).then_inc(max_ready, 1)

                def keep_flip(it, qb, h):
                    g, key0 = group(qb)
                    hi = qb + 1 if g == 0 else GB
                    dve.wait_ge(flipped0, it * FLIPS + flips_before(qb) + (h if g else 0) + 1)
                    at = P * (qb % GB)
                    dve.tensor_copy(probs_T[:, h, key0:key0 + hi, at:at + P],
                                    flip[0][:, 0:P * hi].rearrange("p (k q) -> p k q", q=P)).then_inc(flip0_kept, 1)

                def invert(it, g):
                    dve.wait_ge(probs_ready, it * SCORES + 2 * GB * (g + 1) + CREDIT)
                    dve.wait_ge(recip_flipped, it * QG + g + CREDIT)
                    dve.reciprocal(recip[:], row_sum[:, 2 * GB * g:2 * GB * (g + 1)]).then_inc(recip_step, 1)
                    dve.wait_ge(recip_step, it * QG + g + 1)
                    dve.tensor_copy(recip_x[:], recip[:].unsqueeze(2).broadcast_to([P, 2 * GB, D])).then_inc(recip_ready, 1)

                def normalise(it, n, g):
                    dve.wait_ge(recipT_kept, it * QG + g + 1 + CREDIT)
                    dve.wait_ge(pv_ready, it * QG + g + 1)
                    dve.tensor_tensor(att_T[:, bass.ds(n, 1), 512 * g:512 * (g + 1)].rearrange("p a q -> p (a q)"),
                                      accum[:], recip_T[:], ALU.mult).then_inc(att_kept, 1)

                def begin(it, n):
                    for qb in range(2):
                        for h in range(2):
                            maximum(it, qb, h)
                    dve.wait_ge(v_made, it + 1 + CREDIT)
                    for f in range(2):
                        dve.tensor_tensor(v_sb[:, GB * f:GB * (f + 1), :], flip[f][:].rearrange("p (r d) -> p r d", r=GB),
                                          bv_bc[:, bass.ds(n * 2 * D, 2 * D)].unsqueeze(1).broadcast_to([P, GB, 2 * D]),
                                          ALU.add).then_inc(v_kept, 1)

                def unit(it, n, more):
                    for qb in range(2):
                        keep_flip(it, qb, 0)
                        for h in range(2):
                            maximum(it, qb + 2, h)
                    keep_flip(it, 2, 0)
                    maximum(it, 4, 0)
                    keep_flip(it, 3, 0)
                    maximum(it, 4, 1)
                    invert(it, 0)
                    maximum(it, 5, 0)
                    normalise(it, n, 0)
                    keep_flip(it, 4, 0)
                    maximum(it, 5, 1)
                    keep_flip(it, 4, 1)
                    for qb in range(5, ROWS - 1):
                        for h in range(2):
                            maximum(it, qb + 1, h)
                            keep_flip(it, qb, h)
                    for h in range(2):
                        if more:
                            keep_rest(it + 1, n + 1, h, 0)
                        keep_flip(it, ROWS - 1, h)
                    invert(it, 1)
                    if more:
                        for h in range(2):
                            keep_rest(it + 1, n + 1, h, 1)
                    normalise(it, n, 1)
                    if more:
                        begin(it + 1, n + 1)

                with dve.Fori(0, B) as b:
                    dve.wait_ge(xn_flipped0, b + 1)
                    dve.tensor_copy(xnT[:, 0:512], flip[0][:]).then_inc(xnT_dve, 1)
                    for c in range(2):
                        for h in range(2):
                            keep_rest(b * PAIRS, 0, h, c)
                    for j in range(NHID):
                        dve.wait_ge(silu_ready, b * NHID + j + 1)
                        dve.wait_ge(up_ready, b * NHID + j + 1)
                        dve.tensor_tensor(hid_T[:, j, :], pair[1][:], act_gate[:], ALU.mult).then_inc(hid_kept, 1)
                    begin(b * PAIRS, 0)
                    with dve.Fori(0, PAIRS - 1) as n:
                        unit(b * PAIRS + n, n, True)
                    unit(b * PAIRS + PAIRS - 1, PAIRS - 1, False)
                    dve.wait_ge(xob_ready, b + 1)
                    for f in range(2):
                        dve.wait_ge(branch_ready, 2 * b + f + 1)
                        rows = x1[:, bass.ds(b, 1), GB * f:GB * (f + 1), :].rearrange("p a r e -> p (a r e)")
                        dve.tensor_tensor(rows, flip[f][:], rows, ALU.add).then_inc(x1_kept, 1)

            @block.tensor
            def _(pe):
                pe.sem_inc(v_made, CREDIT)
                pe.sem_inc(xn_flipped1, CREDIT)
                pe.sem_inc(recip_flipped, CREDIT)
                pe.wait_ge(ident_made, 1)
                pe.wait_ge(ints_scaled, 1)
                pe.wait_ge(stage_loaded, 16 * 7)
                for w in range(2):
                    for j in range(NHID):
                        pe.transpose(pair[0][:, w * HID + j * P:w * HID + (j + 1) * P], raw_f[:, w, j * P:(j + 1) * P], ident[:])
                for j in range(NHID):
                    pe.transpose(pair[1][:, j * P:(j + 1) * P], raw_f[:, 2, j * P:(j + 1) * P], ident[:])
                pe.transpose(pair[1][:, 512:512 + COLUMNS], stage[:], ident[0:COLUMNS, 0:COLUMNS]).then_inc(setup_flipped, 1)
                pe.wait_ge(mask_made, 2)
                pe.wait_ge(setup_copied, 4)

                def project(it, h, c):
                    if c:
                        pe.wait_ge(lo_kept, 4 * it + h + 1)
                    for half in range(2):
                        last = pe.matmul(pair[h][:, 512 * half:512 * (half + 1)],
                                         lhsT=w_qk[:, c, h, :, :].rearrange("p c d -> p (c d)"),
                                         rhs=xnT[:, 512 * half:512 * (half + 1)], start=True, stop=True)
                    last.then_inc(proj_made, 1)

                def project_values(it):
                    for r in range(ROWS):
                        last = pe.matmul(flip[r // GB][:, P * (r % GB):P * (r % GB + 1)], lhsT=xnT[:, P * r:P * (r + 1)],
                                         rhs=w_v[:].rearrange("p h d -> p (h d)"), start=True, stop=True)
                    last.then_inc(v_made, 1)

                def score(it, qb, h):
                    if qb < 2:
                        pe.wait_ge(lo_kept, 4 * it + 2 + h + 1)
                    elif qb < GB:
                        pe.wait_ge(probs_ready, it * SCORES + 2 * (qb - 2) + h + 1 + CREDIT)
                    else:
                        pe.wait_ge(probs_ready, it * SCORES + 2 * (qb - 1) + h + 1 + CREDIT)
                    L = P * (qb + 1)
                    at = columns_of(qb).start
                    for lo in range(0, L, 512):
                        w = max(2 * P, min(512, L - lo))
                        for k, part in enumerate((k_hi, k_lo)):
                            pe.matmul(pair[h][:, at + lo:at + lo + w], lhsT=q_st[h][:, P * qb:P * (qb + 1)],
                                      rhs=part[h][:, lo:lo + w], start=k == 0, stop=k == 1 and lo + 512 < L)
                    pe.matmul(pair[h][:, at + L - P:at + L], lhsT=ident_bf[:], rhs=mask[:], start=False, stop=True
                              ).then_inc(scores_ready, 1)

                def flip_probs(it, qb, h):
                    pe.wait_ge(probs_ready, it * SCORES + 2 * qb + h + 1 + CREDIT)
                    at0 = it * FLIPS + flips_before(qb) + CREDIT
                    todo = [(h, at0, 0, qb + 1)] if qb < GB else [(0, at0 + h, 0, GB), (1, at0 + h, GB, qb + 1)]
                    for f, before, lo, hi in todo:
                        pe.wait_ge((flip0_kept, flip1_kept)[f], before)
                        for k in range(lo, hi):
                            last = pe.transpose(flip[f][:, P * (k - lo):P * (k - lo + 1)],
                                                probs[:, h, qb % 2, P * k:P * (k + 1)], ident[:])
                        last.then_inc((flipped0, flipped1)[f], 1)

                def flip_recip(it, g):
                    pe.wait_ge(recip_ready, it * QG + g + 1)
                    pe.wait_ge(recipT_kept, it * QG + g + CREDIT)
                    for qb in range(GB):
                        last = pe.transpose(misc[:, P * qb:P * (qb + 1)],
                                            recip_x[:, 2 * qb:2 * qb + 2, :].rearrange("p h d -> p (h d)"), ident[:])
                    last.then_inc(recip_flipped, 1)

                def weigh(it, g):
                    done = it * FLIPS + flips_before(GB * (g + 1)) + CREDIT
                    pe.wait_ge(flip0_kept, done)
                    pe.wait_ge(flip1_kept, done)
                    pe.wait_ge(att_kept, it * QG + g + CREDIT)
                    keys, key0 = GB * (g + 1), group(g * GB)[1]
                    for k in range(keys):
                        at = P * max(0, k - GB * g)
                        for h in range(2):
                            last = pe.matmul(accum[D * h:D * (h + 1), at:512], lhsT=v_sb[:, k, D * h:D * (h + 1)],
                                             rhs=probs_T[:, h, key0 + k, at:512], start=k == 0, stop=k == keys - 1)
                    last.then_inc(pv_ready, 1)

                def begin(it):
                    for qb in range(2):
                        for h in range(2):
                            score(it, qb, h)
                    project_values(it)

                def unit(it, more):
                    pe.wait_ge(v_kept, 2 * (it + 1))
                    for qb in range(2):
                        for h in range(2):
                            flip_probs(it, qb, h)
                        for h in range(2):
                            score(it, qb + 2, h)
                    for h in range(2):
                        flip_probs(it, 2, h)
                    for h in range(2):
                        score(it, 4, h)
                        flip_probs(it, 3, h)
                    score(it, 5, 0)
                    flip_recip(it, 0)
                    weigh(it, 0)
                    flip_probs(it, 4, 0)
                    score(it, 5, 1)
                    flip_probs(it, 4, 1)
                    for qb in range(5, ROWS - 1):
                        for h in range(2):
                            score(it, qb + 1, h)
                            flip_probs(it, qb, h)
                    if more:
                        pe.wait_ge(q_scaled, it + 2)
                    for h in range(2):
                        if more:
                            pe.wait_ge(probs_ready, it * SCORES + 2 * (ROWS - 1) + h + 1 + CREDIT)
                            project(it + 1, h, 0)
                        flip_probs(it, ROWS - 1, h)
                    if more:
                        project(it + 1, 0, 1)
                    flip_recip(it, 1)
                    if more:
                        project(it + 1, 1, 1)
                    weigh(it, 1)
                    if more:
                        begin(it + 1)

                with pe.Fori(0, B) as b:
                    pe.wait_ge(xn_placed, b + 1)
                    pe.wait_ge(x1_kept, 2 * b + CREDIT)
                    for r in range(ROWS):
                        last = pe.transpose(flip[r // GB][:, P * (r % GB):P * (r % GB + 1)], xn[:, r, :], ident[:])
                        if r == GB - 1:
                            last.then_inc(xn_flipped0, 1)
                    last.then_inc(xn_flipped1, 1)
                    pe.wait_ge(xnT_dve, b + 1)
                    pe.wait_ge(xnT_act, b + 1)
                    pe.wait_ge(q_scaled, b * PAIRS + 1)
                    for c in range(2):
                        for h in range(2):
                            project(b * PAIRS, h, c)
                    for j in range(NHID):
                        for h, w_T in enumerate((gate_T, up_T)):
                            if j == 0:
                                pe.wait_ge(lo_kept, 4 * PAIRS * b + 2 + h + 1)
                            elif h == 0:
                                pe.wait_ge(silu_ready, b * NHID + j)
                            else:
                                pe.wait_ge(hid_kept, b * NHID + j + CREDIT)
                            for half in range(2):
                                last = pe.matmul(pair[h][:, 512 * half:512 * (half + 1)], lhsT=w_T[:, P * j:P * (j + 1)],
                                                 rhs=xnT[:, 512 * half:512 * (half + 1)], start=True, stop=True)
                            last.then_inc((gate_ready, up_ready)[h], 1)
                    pe.wait_ge(silu_ready, (b + 1) * NHID)
                    pe.wait_ge(hid_kept, (b + 1) * NHID + CREDIT)
                    begin(b * PAIRS)
                    with pe.Fori(0, PAIRS - 1) as n:
                        unit(b * PAIRS + n, True)
                    unit(b * PAIRS + PAIRS - 1, False)
                    pe.wait_ge(outw_loaded, 16)
                    pe.wait_ge(att_kept, (b + 1) * PAIRS * QG + CREDIT)
                    for r in range(ROWS):
                        dst = flip[r // GB][:, P * (r % GB):P * (r % GB + 1)]
                        for n2 in range(PAIRS):
                            pe.matmul(dst, lhsT=att_T[:, n2, P * r:P * (r + 1)], rhs=outw_sb[:, n2, :], start=n2 == 0, stop=False)
                        for j in range(NHID):
                            last = pe.matmul(dst, lhsT=hid_T[:, j, P * r:P * (r + 1)], rhs=down_T[:, P * j:P * (j + 1)],
                                             start=False, stop=j == NHID - 1)
                        if r % GB == GB - 1:
                            last.then_inc(branch_ready, 1)


def layer1(nc, sem, sbuf, kept, W1, W2, late, out):
    pair, flip, accum, misc, x1, ident, columns, minus_half, eps = kept
    slow_sb, wout_sb, wg_sb, b2_sb, late_loaded = late
    b1_col, lnw_col, lnb_col = columns[:, 2 * H:2 * H + X * NXB], columns[:, COLUMNS - 2:COLUMNS - 1], columns[:, COLUMNS - 1:COLUMNS]
    HD = H * D
    PARTS = 3 * B
    XS = X // B
    ctx = ExitStack()
    with ctx:
        def sb(name, shape, dt=F32):
            return sbuf(name, shape, dt, ctx)

        w1_sb = sb("w1_sb", [P, X, XH])
        w2_sb = sb("w2_sb", [P, X, NXB, E])
        experts_loaded = sem("experts_loaded")
        stats1 = sb("stats1", [P, B, 6])
        mv_n, mv_h = sb("mv_n", [P, B, 2]), sb("mv_h", [P, B, 2])
        rstd_n, rstd_h = sb("rstd_n", [P, B]), sb("rstd_h", [P, B])
        nrm = sb("nrm", [P, B, E])
        hat = sb("hat", [P, B, E])
        resid = sb("resid", [P, B, E])
        nrm_T = sb("nrm_T", [P, B * P])
        h_T = sb("h_T", [P, B * P])
        sig = sb("sig", [P, 2, B * H])
        beta = sb("beta", [P, B, H])
        gate = sb("gate", [P, B, X])
        stat4 = sb("stat4", [P, 4, B])
        above = sb("above", [P, B, X, X])
        equal = sb("equal", [P, B, X, X])
        earlier = sb("earlier", [P, X, X])
        rank = sb("rank", [P, B, X])
        score = sb("score", [P, B, X])
        score_T = sb("score_T", [X, B * P])
        e_buf = sb("e_buf", [P, 2, HD])
        qs = sb("qs", [P, B, HD])
        ks = sb("ks", [P, B, HD])
        vb = sb("vb", [P, B, HD])
        r_q, r_k = sb("r_q", [P, B, H]), sb("r_k", [P, B, H])
        rk_beta = sb("rk_beta", [P, B, H])
        prod = sb("prod", [P, 2 * B - 1, HD])
        coef = sb("coef", [P, 2 * B - 1, H])
        delta = sb("delta", [P, B, HD])
        part = sb("part", [P, B, HD])
        outs = sb("outs", [P, 2, HD])
        outs_T = sb("outs_T", [P, 2, PAIRS, P])
        hid = sb("hid", [P, NXB, B * P])
        moe = sb("moe", [P, B, E])
        fin = sb("fin", [P, B, E])

        earlier_step, earlier_made = sem("earlier_step"), sem("earlier_made")
        d_step, g_step = sem("d_step"), sem("g_step")
        varn_ready, rstdn_ready, varh_ready, rstdh_ready = sem("varn_ready"), sem("rstdn_ready"), sem("varh_ready"), sem("rstdh_ready")
        eps_step = sem("eps_step")
        nrm_ready, hat_ready, resid_ready = sem("nrm_ready"), sem("hat_ready"), sem("resid_ready")
        nrm_flipped, hat_flipped, nrmT_kept, hT_kept = sem("nrm_flipped"), sem("hat_flipped"), sem("nrmT_kept"), sem("hT_kept")
        small_ready, beta_low, beta_exp = sem("small_ready"), sem("beta_low"), sem("beta_exp")
        logit_ready, gate_exp = sem("logit_ready"), sem("gate_exp_l1")
        score_ready, score_flipped, scoreT_kept = sem("score_ready"), sem("score_flipped"), sem("scoreT_kept")
        part_ready, low_ready, e_ready, part_kept = sem("part_ready"), sem("low_ready"), sem("e_ready"), sem("part_kept")
        hid_ready, hid_kept = sem("hid_ready"), sem("hid_kept_l1")
        y_ready, y_kept = sem("y_ready"), sem("y_kept")
        prod_ready, prod_used = sem("prod_ready"), sem("prod_used")
        terms_ready, out_step, out_ready = sem("terms_ready"), sem("out_step"), sem("out_ready")
        out_flipped, outT_kept = sem("out_flipped"), sem("outT_kept")
        attn_ready, fin_ready, stored = sem("attn_ready"), sem("fin_ready"), sem("stored")

        out_v = out.rearrange("s (t p) e -> t p s e", p=P)

        def heads(ap):
            return ap.rearrange("p (h d) -> p h d", h=H)

        def over_heads(ap):
            return ap.unsqueeze(len(ap.shape)).broadcast_to([*ap.shape, D])

        with nc.Block() as block:

            @block.sync
            def _(sp):
                sp.dma_start(w1_sb[:], W1.rearrange("x e h -> e x h")).then_inc(experts_loaded, 16)
                sp.dma_start(w2_sb[:], W2.rearrange("x (j p) e -> p x j e", p=P)).then_inc(experts_loaded, 16)
                with sp.Fori(0, ROWS) as t:
                    sp.wait_ge(fin_ready, t + 1)
                    sp.dma_start(out_v[t], fin[:]).then_inc(stored, 16)
                sp.wait_ge(stored, 16 * ROWS)

            @block.gpsimd
            def _(pool):
                pool.memset(earlier[:], 1.0).then_inc(earlier_step, 1)
                pool.wait_ge(earlier_step, 1)
                pool.affine_select(out=earlier[:], in_=earlier[:], compare_op=ALU.is_gt, fill=0.0, base=0,
                                   pattern=[[1, X], [-1, X]], channel_multiplier=0).then_inc(earlier_made, 1)
                with pool.Fori(0, ROWS) as t:
                    for k, (ready, mv, rstd, done) in enumerate(((varn_ready, mv_n, rstd_n, rstdn_ready),
                                                                 (varh_ready, mv_h, rstd_h, rstdh_ready))):
                        pool.wait_ge(ready, t + 1)
                        pool.tensor_tensor(rstd[:], mv[:, :, 1], eps[:, 0:B], ALU.add).then_inc(eps_step, 1)
                        pool.wait_ge(eps_step, 2 * t + k + 1)
                        pool.tensor_tensor(rstd[:], rstd[:], minus_half[:, 0:B], ALU.pow).then_inc(done, 1)
                    pool.wait_ge(fin_ready, t)
                    pool.wait_ge(nrm_ready, t + 1)
                    pool.tensor_tensor(resid[:], nrm[:], x1[:, :, bass.ds(t, 1), :].rearrange("p s a e -> p s (a e)"),
                                       ALU.add).then_inc(resid_ready, 1)

                    def products(s):
                        pool.wait_ge(part_kept, PARTS * t + 3 * s + 2)
                        pool.wait_ge(prod_used, B * t + s)
                        if s:
                            pool.tensor_tensor(prod[:, 0:s, :], ks[:, 0:s, :],
                                               ks[:, s:s + 1, :].broadcast_to([P, s, HD]), ALU.mult).then_inc(prod_ready, 1)
                        pool.tensor_tensor(prod[:, B - 1:B + s, :], ks[:, 0:s + 1, :],
                                           qs[:, s:s + 1, :].broadcast_to([P, s + 1, HD]), ALU.mult).then_inc(prod_ready, 1)

                    def sums(s):
                        base = t * (B * (B - 1) // 2 - (B - 1)) + (s - 1) * (s - 2) // 2
                        pool.wait_ge(terms_ready, B * t + s + 1)
                        pool.wait_ge(out_flipped, B * t + max(s - 1, 0))
                        for k in range(1, s + 1):
                            if k > 1:
                                pool.wait_ge(out_step, base + k - 1)
                            first = part[:, 0, :] if k == 1 else outs[:, s % 2, :]
                            pool.tensor_tensor(outs[:, s % 2, :], first, part[:, k, :], ALU.add
                                               ).then_inc(out_ready if k == s else out_step, 1)

                    products(0)
                    products(1)
                    for s in range(2, B):
                        products(s)
                        if s > 2:
                            sums(s - 2)
                    sums(B - 2)
                    sums(B - 1)

            @block.scalar
            def _(act):
                with act.Fori(0, ROWS) as t:
                    act.wait_ge(nrm_flipped, t + 1)
                    act.activation(nrm_T[:], flip[0][:], ACT.Copy).then_inc(nrmT_kept, 1)
                    act.wait_ge(hat_flipped, t + 1)
                    act.activation(h_T[:], flip[1][:], ACT.Identity, bias=lnb_col, scale=lnw_col).then_inc(hT_kept, 1)
                    act.wait_ge(small_ready, t + 1)
                    act.activation(sig[:, 0, :], misc[:, 0:B * H], ACT.Relu, scale=-1.0).then_inc(beta_low, 1)
                    act.activation(sig[:, 1, :], misc[:, 0:B * H], ACT.Abs).then_inc(beta_low, 1)
                    act.wait_ge(beta_low, 2 * t + 2)
                    act.activation(sig[:], sig[:], ACT.Exp, scale=-1.0).then_inc(beta_exp, 1)
                    act.wait_ge(logit_ready, t + 1)
                    act.activation(gate[:], gate[:], ACT.Exp).then_inc(gate_exp, 1)

                    def exps(s):
                        for k in range(2):
                            n = 3 * s + k
                            act.wait_ge(part_ready, PARTS * t + n + 1)
                            if s:
                                act.wait_ge(part_kept, PARTS * t + n - 2)
                            act.activation(e_buf[:, k, :], pair[n % 2][:], ACT.Relu, scale=-1.0).then_inc(low_ready, 1)
                            act.wait_ge(low_ready, 2 * B * t + 2 * s + k + 1)
                            act.activation(e_buf[:, k, :], e_buf[:, k, :], ACT.Exp, scale=-1.0).then_inc(e_ready, 1)

                    def relus(e):
                        for j in range(NXB):
                            act.wait_ge(hid_ready, X * NXB * t + NXB * e + j + 1)
                            act.wait_ge(y_ready, X * t + e)
                            act.activation(hid[:, j, :], flip[j][:], ACT.Relu,
                                           bias=b1_col[:, NXB * e + j:NXB * e + j + 1]).then_inc(hid_kept, 1)

                    for s in range(B):
                        exps(s)
                        for e in range(XS * s, XS * (s + 1)):
                            relus(e)
                    act.wait_ge(score_flipped, t + 1)
                    act.activation(score_T[:], misc[0:X, :], ACT.Copy).then_inc(scoreT_kept, 1)
                    for s in range(B):
                        act.wait_ge(out_flipped, B * t + s + 1)
                        act.activation(outs_T[:, s % 2, :, :].rearrange("p n q -> p (n q)"), pair[s % 2][:], ACT.Copy
                                       ).then_inc(outT_kept, 1)

            @block.vector
            def _(dve):
                with dve.Fori(0, ROWS) as t:
                    count = [0, 0]

                    def link(op):
                        op.then_inc(d_step, 1)
                        count[0] += 1
                        dve.wait_ge(d_step, D_STEPS * t + count[0])

                    D_STEPS = 47

                    def norm(src, dst, mv, rstd, ready, rstd_ready, done):
                        for s in range(B):
                            last = dve.bn_stats(stats1[:, s, :], src(s))
                        link(last)
                        dve.memset(eps[:, 0:B], EPS)
                        for s in range(B):
                            last = dve.bn_aggr(mv[:, s, :], stats1[:, s, :])
                        last.then_inc(ready, 1)
                        dve.wait_ge(rstd_ready, t + 1)
                        for s in range(B):
                            last = dve.tensor_scalar(dst[:, s, :], src(s), mv[:, s, 0:1], rstd[:, s:s + 1],
                                                     ALU.subtract, ALU.mult)
                        last.then_inc(done, 1)

                    norm(lambda s: x1[:, s, bass.ds(t, 1), :].rearrange("p a e -> p (a e)"), nrm, mv_n, rstd_n,
                         varn_ready, rstdn_ready, nrm_ready)
                    dve.wait_ge(nrm_ready, t + 1)
                    norm(lambda s: nrm[:, s, :], hat, mv_h, rstd_h, varh_ready, rstdh_ready, hat_ready)

                    dve.wait_ge(beta_exp, t + 1)
                    link(dve.tensor_scalar(sig[:, 1, :], sig[:, 1, :], 1.0, None, ALU.add))
                    link(dve.reciprocal(sig[:, 1, :], sig[:, 1, :]))
                    link(dve.tensor_tensor(beta[:].rearrange("p s h -> p (s h)"), sig[:, 0, :], sig[:, 1, :], ALU.mult))

                    mx, total, top_sum, inv = (stat4[:, k, :] for k in range(4))

                    def over(ap):
                        return ap.unsqueeze(2).broadcast_to([P, B, X])

                    logits = misc[:, B * H:B * (H + X)].rearrange("p (s x) -> p s x", s=B)
                    dve.wait_ge(small_ready, t + 1)
                    link(dve.tensor_reduce(out=mx, in_=logits, axis=AX.X, op=ALU.max))
                    dve.tensor_tensor(gate[:], logits, over(mx), ALU.subtract).then_inc(logit_ready, 1)
                    dve.wait_ge(gate_exp, t + 1)
                    link(dve.tensor_reduce(out=total, in_=gate[:], axis=AX.X, op=ALU.add))
                    link(dve.reciprocal(inv, total))
                    link(dve.tensor_tensor(gate[:], gate[:], over(inv), ALU.mult))
                    mine = gate[:].unsqueeze(3).broadcast_to([P, B, X, X])
                    other = gate[:].unsqueeze(2).broadcast_to([P, B, X, X])
                    dve.tensor_tensor(above[:], other, mine, ALU.is_gt)
                    link(dve.tensor_tensor(equal[:], other, mine, ALU.is_equal))
                    dve.wait_ge(earlier_made, 1)
                    link(dve.tensor_tensor(equal[:], equal[:], earlier[:].unsqueeze(1).broadcast_to([P, B, X, X]), ALU.mult))
                    link(dve.tensor_tensor(above[:], above[:], equal[:], ALU.add))
                    link(dve.tensor_reduce(out=rank[:], in_=above[:], axis=AX.X, op=ALU.add))
                    link(dve.scalar_tensor_tensor(rank[:], rank[:], float(TOP), gate[:], ALU.is_lt, ALU.mult))
                    link(dve.tensor_reduce(out=top_sum, in_=rank[:], axis=AX.X, op=ALU.add))
                    link(dve.reciprocal(inv, top_sum))
                    dve.tensor_tensor(score[:], rank[:], over(inv), ALU.mult).then_inc(score_ready, 1)
                    dve.wait_ge(score_ready, t + 1)

                    def keep(s):
                        for k, dst in ((0, qs), (1, ks)):
                            dve.wait_ge(e_ready, 2 * B * t + 2 * s + k + 1)
                            n = 3 * s + k
                            dve.scalar_tensor_tensor(dst[:, s, :], pair[n % 2][:], 0.0, e_buf[:, k, :],
                                                     ALU.max, ALU.add).then_inc(part_kept, 1)
                        n = 3 * s + 2
                        dve.wait_ge(part_ready, PARTS * t + n + 1)
                        dve.tensor_tensor(heads(vb[:, s, :]), heads(pair[n % 2][:]), over_heads(beta[:, s, :]),
                                          ALU.mult).then_inc(part_kept, 1)
                        dve.wait_ge(part_kept, PARTS * t + 3 * s + 2)
                        dve.tensor_reduce(out=r_q[:, s, :], in_=heads(qs[:, s, :]), axis=AX.X, op=ALU.add)
                        link(dve.tensor_reduce(out=r_k[:, s, :], in_=heads(ks[:, s, :]), axis=AX.X, op=ALU.add))
                        dve.reciprocal(r_q[:, s, :], r_q[:, s, :])
                        link(dve.reciprocal(r_k[:, s, :], r_k[:, s, :]))
                        link(dve.tensor_tensor(rk_beta[:, s, :], r_k[:, s, :], beta[:, s, :], ALU.mult))

                    def gather(e):
                        dve.wait_ge(y_ready, X * t + e + 1)
                        for s in range(B):
                            src = accum[:, P * s:P * (s + 1)]
                            if e == 0:
                                last = dve.tensor_scalar(moe[:, s, :], src, score[:, s, e:e + 1], None, ALU.mult)
                            else:
                                last = dve.scalar_tensor_tensor(moe[:, s, :], src, score[:, s, e:e + 1], moe[:, s, :],
                                                                ALU.mult, ALU.add)
                        last.then_inc(y_kept, 1)

                    def scan(s):
                        dve.wait_ge(prod_ready, (2 * B - 1) * t + 2 * s + 1)
                        dve.wait_ge(terms_ready, B * t + s)
                        if s:
                            dve.tensor_reduce(out=coef[:, 0:s, :], in_=prod[:, 0:s, :].rearrange("p s (h d) -> p s h d", h=H),
                                              axis=AX.X, op=ALU.add)
                        red = dve.tensor_reduce(out=coef[:, B - 1:B + s, :],
                                                in_=prod[:, B - 1:B + s, :].rearrange("p s (h d) -> p s h d", h=H),
                                                axis=AX.X, op=ALU.add)
                        red.then_inc(prod_used, 1)
                        dve.wait_ge(prod_used, B * t + s + 1)
                        if s:
                            dve.tensor_tensor(coef[:, 0:s, :], coef[:, 0:s, :], r_k[:, 0:s, :], ALU.mult)
                        link(dve.tensor_tensor(coef[:, B - 1:B + s, :], coef[:, B - 1:B + s, :], r_k[:, 0:s + 1, :], ALU.mult))
                        if s:
                            dve.tensor_tensor(coef[:, 0:s, :], coef[:, 0:s, :],
                                              rk_beta[:, s:s + 1, :].broadcast_to([P, s, H]), ALU.mult)
                        link(dve.tensor_tensor(coef[:, B - 1:B + s, :], coef[:, B - 1:B + s, :],
                                               r_q[:, s:s + 1, :].broadcast_to([P, s + 1, H]), ALU.mult))
                        if s:
                            if s > 1:
                                dve.wait_ge(out_ready, (B - 1) * t + s - 1)
                            link(dve.tensor_tensor(part[:, 0:s, :].rearrange("p s (h d) -> p (s h) d", h=H),
                                                   delta[:, 0:s, :].rearrange("p s (h d) -> p (s h) d", h=H),
                                                   over_heads(coef[:, 0:s, :].rearrange("p s h -> p (s h)")), ALU.mult))
                            for k in range(s):
                                first = vb[:, s, :] if k == 0 else delta[:, s, :]
                                link(dve.tensor_tensor(delta[:, s, :], first, part[:, k, :], ALU.subtract))
                        else:
                            link(dve.tensor_copy(delta[:, 0, :], vb[:, 0, :]))
                        dst = part[:, 0:s + 1, :].rearrange("p s (h d) -> p (s h) d", h=H)
                        if s == 0:
                            dst = heads(outs[:, 0, :])
                        dve.tensor_tensor(dst, delta[:, 0:s + 1, :].rearrange("p s (h d) -> p (s h) d", h=H),
                                          over_heads(coef[:, B - 1:B + s, :].rearrange("p s h -> p (s h)")), ALU.mult
                                          ).then_inc(terms_ready, 1)

                    for s in range(2):
                        keep(s)
                        for e in range(XS * s, XS * (s + 1)):
                            gather(e)
                    scan(0)
                    for s in range(2, B):
                        keep(s)
                        for e in range(XS * s, XS * (s + 1)):
                            gather(e)
                        scan(s - 1)
                    scan(B - 1)

                    dve.wait_ge(y_kept, X * (t + 1))
                    dve.wait_ge(attn_ready, t + 1)
                    dve.wait_ge(stored, 16 * t)
                    link(dve.tensor_tensor(fin[:].rearrange("p s e -> p (s e)"), accum[:], moe[:].rearrange("p s e -> p (s e)"), ALU.add))
                    dve.wait_ge(resid_ready, t + 1)
                    dve.tensor_tensor(fin[:], fin[:], resid[:], ALU.add).then_inc(fin_ready, 1)
                    assert count[0] == D_STEPS, count

            @block.tensor
            def _(pe):
                pe.wait_ge(late_loaded, 16 * 4)
                pe.wait_ge(experts_loaded, 32)
                with pe.Fori(0, ROWS) as t:
                    pe.wait_ge(nrm_ready, t + 1)
                    pe.wait_ge(hid_kept, X * NXB * t)
                    for s in range(B):
                        last = pe.transpose(flip[0][:, P * s:P * (s + 1)], nrm[:, s, :], ident[:])
                    last.then_inc(nrm_flipped, 1)
                    pe.wait_ge(hat_ready, t + 1)
                    for s in range(B):
                        last = pe.transpose(flip[1][:, P * s:P * (s + 1)], hat[:, s, :], ident[:])
                    last.then_inc(hat_flipped, 1)
                    pe.wait_ge(nrmT_kept, t + 1)
                    pe.wait_ge(hT_kept, t + 1)
                    pe.wait_ge(scoreT_kept, t)
                    for s in range(B):
                        rows = slice(P * s, P * (s + 1))
                        pe.matmul(misc[:, H * s:H * (s + 1)], lhsT=h_T[:, rows], rhs=slow_sb[:, :, 3 * D], start=True, stop=True)
                    for s in range(B):
                        rows = slice(P * s, P * (s + 1))
                        last = pe.matmul(misc[:, B * H + X * s:B * H + X * (s + 1)], lhsT=nrm_T[:, rows], rhs=wg_sb[:],
                                         start=True, stop=True)
                    last.then_inc(small_ready, 1)

                    def project(s):
                        for c in range(3):
                            n = 3 * s + c
                            if n >= 2:
                                pe.wait_ge(part_kept, PARTS * t + n - 1)
                            else:
                                pe.wait_ge(outT_kept, B * t)
                            for half in range(2):
                                last = pe.matmul(pair[n % 2][:, 512 * half:512 * (half + 1)], lhsT=h_T[:, P * s:P * (s + 1)],
                                                 rhs=slow_sb[:, 8 * half:8 * (half + 1), c * D:(c + 1) * D],
                                                 start=True, stop=True)
                            last.then_inc(part_ready, 1)

                    def expert(e):
                        for j in range(NXB):
                            pe.wait_ge(hid_kept, X * NXB * t + max(NXB * (e - 1) + j + 1, 0))
                            pe.matmul(flip[j][:], lhsT=w1_sb[:, e, P * j:P * (j + 1)], rhs=nrm_T[:], start=True,
                                      stop=True).then_inc(hid_ready, 1)
                        pe.wait_ge(hid_kept, X * NXB * t + NXB * (e + 1))
                        if e:
                            pe.wait_ge(y_kept, X * t + e)
                        else:
                            pe.wait_ge(fin_ready, t)
                        for s in range(B):
                            for j in range(NXB):
                                last = pe.matmul(accum[:, P * s:P * (s + 1)], lhsT=hid[:, j, P * s:P * (s + 1)],
                                                 rhs=w2_sb[:, e, j, :], start=j == 0, stop=j == NXB - 1)
                        last.then_inc(y_ready, 1)

                    for s in range(B):
                        project(s)
                        for e in range(XS * s, XS * (s + 1)):
                            expert(e)

                    pe.wait_ge(score_ready, t + 1)
                    for s in range(B):
                        last = pe.transpose(misc[0:X, P * s:P * (s + 1)], score[:, s, :], ident[:])
                    last.then_inc(score_flipped, 1)

                    def flip_out(s):
                        if s == 0:
                            pe.wait_ge(terms_ready, B * t + 1)
                        else:
                            pe.wait_ge(out_ready, (B - 1) * t + s)
                        if s >= 2:
                            pe.wait_ge(outT_kept, B * t + s - 1)
                        else:
                            pe.wait_ge(part_kept, PARTS * (t + 1))
                        for n in range(PAIRS):
                            last = pe.transpose(pair[s % 2][:, P * n:P * (n + 1)], outs[:, s % 2, P * n:P * (n + 1)], ident[:])
                        last.then_inc(out_flipped, 1)

                    def join(s):
                        pe.wait_ge(outT_kept, B * t + s + 1)
                        if s == 0:
                            pe.wait_ge(scoreT_kept, t + 1)
                            pe.wait_ge(y_kept, X * (t + 1))
                        dst = accum[:, P * s:P * (s + 1)]
                        pe.matmul(dst, lhsT=score_T[:, P * s:P * (s + 1)], rhs=b2_sb[:], start=True, stop=False)
                        for n in range(PAIRS):
                            last = pe.matmul(dst, lhsT=outs_T[:, s % 2, n, :], rhs=wout_sb[:, n, :], start=False, stop=n == PAIRS - 1)
                        if s == B - 1:
                            last.then_inc(attn_ready, 1)

                    flip_out(0)
                    for s in range(1, B):
                        flip_out(s)
                        join(s - 1)
                    join(B - 1)


_INS = ['L0_attn_x', 'L0_attn_qkv_w', 'L0_attn_qkv_b', 'L0_attn_out_w', 'L0_attn_out_b', 'L0_ffn_w_gate', 'L0_ffn_w_up',
        'L0_ffn_w_down', 'L1_attn_ln_w', 'L1_attn_ln_b', 'L1_attn_w_slow', 'L1_attn_w_out', 'L1_ffn_Wg', 'L1_ffn_W1',
        'L1_ffn_b1', 'L1_ffn_W2', 'L1_ffn_b2']


def kernel(**inputs):
    import numpy as np
    import concourse.bacc as bacc
    from concourse.bass_utils import run_bass_kernel_spmd

    nc = bacc.Bacc("TRN2", target_bir_lowering=False, num_devices=1)
    arrays, args = {}, []
    for name in _INS:
        a = np.ascontiguousarray(inputs[name])
        arrays[f"in_{name}"] = a
        args.append(nc.dram_tensor(f"in_{name}", a.shape, mybir.dt.from_np(a.dtype), kind="ExternalInput").ap())
    out = nc.dram_tensor("out_0", (B, S, E), F32, kind="ExternalOutput").ap()
    block_kernel(nc, *args, out)
    r = run_bass_kernel_spmd(nc, [arrays], core_ids=[0])
    return r.results[0]["out_0"]
```

```python
from contextlib import ExitStack

import concourse.bass as bass
from concourse import mybir

F32 = mybir.dt.float32
F32R = mybir.dt.float32r
BF16 = mybir.dt.bfloat16
I32 = mybir.dt.int32
ALU = mybir.AluOpType
ACT = mybir.ActivationFunctionType
AX = mybir.AxisListType

P = 128
E = 128
B, S = 4, 1024
ROWS = S // P
H, D = 16, 64
PAIRS = H // 2
HID = 384
NHID = HID // P
X, XH, NXB = 8, 256, 2
TOP = 2
QG = 2
GB = ROWS // QG
EPS = 1e-5
SCALE = D ** -0.5
INT_SCALE = 1.0 / 127.0
MASKED = -0.7 * 3.4028234663852886e38
COLUMNS = 2 * H + X * NXB + 2
CREDIT = 1

SCORES = 2 * ROWS
FLIPS = GB + 2 * GB


def flips_before(qb):
    return qb if qb < GB else GB + 2 * (qb - GB)


def block_kernel(nc, x, qkv_w, qkv_b, out_w, out_b, w_gate, w_up, w_down, ln_w, ln_b, w_slow, w_out,
                 Wg, W1, b1, W2, b2, out):
    top = ExitStack()
    with top:
        def sem(name):
            return top.enter_context(nc.semaphore(name))

        def sbuf(name, shape, dt=F32, where=top):
            return where.enter_context(nc.sbuf_tensor(name, shape, dt))

        def psum(name, shape, dt=F32):
            return top.enter_context(nc.psum_tensor(name, shape, dt))

        pair = [psum("pair0", [P, 1024]), psum("pair1", [P, 1024])]
        flip = [psum("flip0", [P, 512]), psum("flip1", [P, 512])]
        accum = psum("accum", [P, 512])
        misc = psum("misc", [P, 512])

        x1 = sbuf("x1", [P, B, ROWS, E])
        ident = sbuf("ident", [P, P])
        columns = sbuf("columns", [P, COLUMNS])
        minus_half = sbuf("minus_half", [P, ROWS])
        eps = sbuf("eps", [P, ROWS])
        slow_sb = sbuf("slow_sb", [P, 3, H * D])
        beta_w = sbuf("beta_w", [P, H])
        wout_sb = sbuf("wout_sb", [P, PAIRS, E])
        wg_sb = sbuf("wg_sb", [P, X])
        b2_sb = sbuf("b2_sb", [X, E])
        late_loaded = sem("late_loaded")

        kept = pair, flip, accum, misc, x1, ident, columns, minus_half, eps
        late = slow_sb, beta_w, wout_sb, wg_sb, b2_sb, late_loaded
        layer0(nc, sem, sbuf, kept, x, qkv_w, qkv_b, out_w, out_b, w_gate, w_up, w_down, ln_w, ln_b,
               w_slow, w_out, Wg, b1, b2, late)
        layer1(nc, sem, sbuf, kept, W1, W2, late, out)


def layer0(nc, sem, sbuf, kept, x, qkv_w, qkv_b, out_w, out_b, w_gate, w_up, w_down, ln_w, ln_b, w_slow, w_out, Wg, b1, b2, late):
    pair, flip, accum, misc, x1, ident, columns, minus_half, eps = kept
    slow_sb, beta_w, wout_sb, wg_sb, b2_sb, late_loaded = late
    bq8, bk = columns[:, 0:H], columns[:, H:2 * H]
    ctx = ExitStack()
    with ctx:
        def sb(name, shape, dt=F32):
            return sbuf(name, shape, dt, ctx)

        ident_bf = sb("ident_bf", [P, P], BF16)
        mask = sb("mask", [P, P], BF16)
        stage = sb("stage", [COLUMNS, P])
        outb_bc = sb("outb_bc", [P, E])
        bv_bc = sb("bv_bc", [P, H * D])
        outw_sb = sb("outw_sb", [P, PAIRS, E])
        gate_T = sb("gate_T", [P, HID])
        up_T = sb("up_T", [P, HID])
        down_T = sb("down_T", [P, HID])
        xn_all = sb("xn_all", [P, B, ROWS, E])
        xn = sb("xn", [P, ROWS, E])
        xnT = sb("xnT", [P, S])
        stats = sb("stats", [P, ROWS, 6])
        mv = sb("mv", [P, ROWS, 2])
        rstd = sb("rstd", [P, ROWS])
        w_qk = sb("w_qk", [P, 2, 2, 2, D])
        w_v = sb("w_v", [P, 2, D])
        q_st = [sb(f"q_st{h}", [P, S], F32R) for h in range(2)]
        k_hi = [sb(f"k_hi{h}", [P, S], F32R) for h in range(2)]
        k_lo = [sb(f"k_lo{h}", [P, S], F32R) for h in range(2)]
        v_sb = sb("v_sb", [P, ROWS, 2 * D])
        neg_max = sb("neg_max", [P, SCORES])
        row_sum = sb("row_sum", [P, SCORES])
        recip = sb("recip", [P, 2 * GB])
        recip_x = sb("recip_x", [P, 2 * GB, D])
        recip_T = sb("recip_T", [P, 512])
        probs = sb("probs", [P, 2, 2, S])
        probs_T = sb("probs_T", [P, 2, ROWS, 512])
        att_T = sb("att_T", [P, PAIRS, S])
        act_gate = sb("act_gate", [P, S])
        hid_T = sb("hid_T", [P, NHID, S])
        raw = att_T[:, 0:2, :].rearrange("p a b -> p (a b)").bitcast(I32)[:, 0:3 * HID] \
            .rearrange("p (w n) -> p w n", w=3)
        raw_f = hid_T[:, 0:2, :].rearrange("p a b -> p (a b)")[:, 0:3 * HID].rearrange("p (w n) -> p w n", w=3)

        zero = sb("zero", [P, E])
        scale_row = sb("scale_row", [P, 4 * D])
        consts_made = sem("consts_made")
        ints_loaded, small_loaded = sem("ints_loaded"), sem("small_loaded")
        stage_loaded, outw_loaded = sem("stage_loaded"), sem("outw_loaded")
        x_loaded, pair_loaded, q_scaled = sem("x_loaded"), sem("pair_loaded"), sem("q_scaled")
        ident_made, mask_made, const_step = sem("ident_made"), sem("mask_made"), sem("const_step")
        ints_scaled, setup_flipped, setup_copied = sem("ints_scaled"), sem("setup_flipped"), sem("setup_copied")
        bq_scaled, dve_step = sem("bq_scaled"), sem("dve_step")
        var_ready, rstd_ready, pool_step = sem("var_ready"), sem("rstd_ready"), sem("pool_step")
        xn_ready, xob_ready, xn_placed = sem("xn_ready"), sem("xob_ready"), sem("xn_placed")
        xn_flipped0, xn_flipped1 = sem("xn_flipped0"), sem("xn_flipped1")
        xnT_dve, xnT_act = sem("xnT_dve"), sem("xnT_act")
        proj_made, hi_kept, lo_kept = sem("proj_made"), sem("hi_kept"), sem("lo_kept")
        v_made, v_kept, low_weighed = sem("v_made"), sem("v_kept"), sem("low_weighed")
        scores_ready, max_ready, probs_ready = sem("scores_ready"), sem("max_ready"), sem("probs_ready")
        flipped0, flipped1 = sem("flipped0"), sem("flipped1")
        flip0_kept, flip1_kept = sem("flip0_kept"), sem("flip1_kept")
        recip_step, recip_ready = sem("recip_step"), sem("recip_ready")
        recip_flipped, recipT_kept = sem("recip_flipped"), sem("recipT_kept")
        pv_ready, att_kept = sem("pv_ready"), sem("att_kept")
        gate_ready, up_ready, silu_ready, hid_kept = sem("gate_ready"), sem("up_ready"), sem("silu_ready"), sem("hid_kept")
        branch_ready, x1_kept = sem("branch_ready"), sem("x1_kept")

        x_v = x.rearrange("b (r p) e -> b p r e", p=P)
        qkv_v = qkv_w.rearrange("e (n h) (c d) -> n e c h d", h=2, c=3)
        qkvb_v = qkv_b.rearrange("h (c d) -> c h d", c=3)

        def group(qb):
            return qb // GB, (GB if qb < GB else 0)

        def columns_of(qb):
            half = 512 * (qb % 2) if qb < GB else 0
            return slice(half, half + P * (qb + 1))

        with nc.Block() as block:

            @block.sync
            def _(sp):
                with sp.Fori(0, B) as b:
                    sp.dma_start(x1[:, bass.ds(b, 1), :, :].rearrange("p a r e -> p (a r) e"), x_v[b]).then_inc(x_loaded, 16)
                for w, src in enumerate((w_gate, w_up)):
                    sp.dma_start(raw[:, w, :].rearrange("p (j e) -> p j e", j=NHID),
                                 src.rearrange("(j p) e -> p j e", p=P)).then_inc(ints_loaded, 16)
                sp.dma_start(raw[:, 2, :], w_down).then_inc(ints_loaded, 16)
                for c in range(2):
                    for copy in range(2):
                        sp.dma_start(stage[c * H:(c + 1) * H, copy * D:(copy + 1) * D], qkvb_v[c]).then_inc(stage_loaded, 16)
                sp.dma_start(stage[2 * H:2 * H + X * NXB, :], b1.rearrange("x (j p) -> (x j) p", p=P)).then_inc(stage_loaded, 16)
                sp.dma_start(stage[COLUMNS - 2:COLUMNS - 1, :], ln_w.unsqueeze(0)).then_inc(stage_loaded, 16)
                sp.dma_start(stage[COLUMNS - 1:COLUMNS, :], ln_b.unsqueeze(0)).then_inc(stage_loaded, 16)
                sp.dma_start(outb_bc[:], out_b.unsqueeze(0).broadcast_to([P, E])).then_inc(small_loaded, 16)
                sp.dma_start(bv_bc[:].rearrange("p (h d) -> p h d", h=H),
                             qkv_b[:, 2 * D:3 * D].unsqueeze(0).broadcast_to([P, H, D])).then_inc(small_loaded, 16)
                with sp.Fori(0, B) as b:
                    with sp.Fori(0, PAIRS) as n:
                        sp.wait_ge(v_made, 2 * (b * PAIRS + n) + CREDIT)
                        for c in range(2):
                            for copy in range(2):
                                sp.dma_start(w_qk[:, c, :, copy, :], qkv_v[n, :, c]).then_inc(pair_loaded, 16)
                        sp.dma_start(w_v[:], qkv_v[n, :, 2]).then_inc(pair_loaded, 16)

            @block.gpsimd
            def _(pool):
                pool.memset(ident[:], 0.0).then_inc(const_step, 1)
                pool.wait_ge(const_step, 1)
                pool.affine_select(out=ident[:], in_=ident[:], compare_op=ALU.not_equal, fill=1.0, base=0,
                                   pattern=[[-1, P]], channel_multiplier=1).then_inc(ident_made, 1)
                pool.memset(minus_half[:], -0.5).then_inc(const_step, 1)
                pool.memset(mask[:], 0.0).then_inc(const_step, 1)
                pool.wait_ge(const_step, 3)
                pool.affine_select(out=mask[:], in_=mask[:], compare_op=ALU.is_ge, fill=MASKED, base=0,
                                   pattern=[[-1, P]], channel_multiplier=1).then_inc(mask_made, 1)
                pool.wait_ge(ident_made, 1)
                pool.tensor_copy(ident_bf[:], ident[:]).then_inc(mask_made, 1)
                with pool.Fori(0, B) as b:
                    pool.wait_ge(var_ready, b + 1)
                    pool.tensor_tensor(rstd[:], mv[:, :, 1], eps[:], ALU.add).then_inc(pool_step, 1)
                    pool.wait_ge(pool_step, b + 1)
                    pool.tensor_tensor(rstd[:], rstd[:], minus_half[:], ALU.pow).then_inc(rstd_ready, 1)
                pool.wait_ge(ints_scaled, 1)
                pool.dma_start(outw_sb[:], out_w.rearrange("(n h) d e -> (h d) n e", h=2)).then_inc(outw_loaded, 16)
                slow_v = w_slow.rearrange("e (h f) -> e h f", h=H)
                for c in range(3):
                    pool.dma_start(slow_sb[:, c, :].rearrange("p (h d) -> p h d", h=H),
                                   slow_v[:, :, c * D:(c + 1) * D]).then_inc(late_loaded, 16)
                pool.dma_start(beta_w[:].unsqueeze(2), slow_v[:, :, 3 * D:3 * D + 1],
                               allow_slow_non_contiguous=True).then_inc(late_loaded, 16)
                pool.dma_start(wout_sb[:], w_out.rearrange("(n p) e -> p n e", p=P)).then_inc(late_loaded, 16)
                pool.dma_start(wg_sb[:], Wg).then_inc(late_loaded, 16)
                pool.dma_start(b2_sb[:], b2).then_inc(late_loaded, 16)
                with pool.Fori(0, B) as b:
                    pool.wait_ge(xn_ready, b + 1)
                    pool.wait_ge(xn_flipped1, b + CREDIT)
                    pool.wait_ge(consts_made, 2)
                    pool.tensor_tensor(xn[:], xn_all[:, bass.ds(b, 1), :, :].rearrange("p a r e -> p (a r) e"),
                                       zero[:].unsqueeze(1).broadcast_to([P, ROWS, E]), ALU.add).then_inc(xn_placed, 1)
                    pool.wait_ge(small_loaded, 32)
                    pool.tensor_tensor(x1[:, bass.ds(b, 1), :, :].rearrange("p a r e -> p (a r) e"),
                                       x1[:, bass.ds(b, 1), :, :].rearrange("p a r e -> p (a r) e"),
                                       outb_bc[:].unsqueeze(1).broadcast_to([P, ROWS, E]), ALU.add).then_inc(xob_ready, 1)
                    with pool.Fori(0, PAIRS) as n:
                        pool.wait_ge(pair_loaded, 80 * (b * PAIRS + n + 1))
                        pool.tensor_tensor(w_qk[:, 0, :, :, :].rearrange("p h c d -> p (h c d)"),
                                           w_qk[:, 0, :, :, :].rearrange("p h c d -> p (h c d)"),
                                           scale_row[:], ALU.mult).then_inc(q_scaled, 1)

            @block.scalar
            def _(act):
                act.sem_inc(probs_ready, CREDIT)
                act.sem_inc(flip1_kept, CREDIT)
                act.sem_inc(recipT_kept, CREDIT)

                def keep_part(it, n, h, c):
                    act.wait_ge(proj_made, 4 * it + 2 * c + h + 1)
                    act.wait_ge(bq_scaled, 1)
                    bias = (bq8, bk)[c]
                    act.activation((q_st, k_hi)[c][h][:], pair[h][:], ACT.Identity, bias=bias[:, bass.ds(2 * n + h, 1)]
                                   ).then_inc(hi_kept, 1)

                def softmax(it, qb, h):
                    i = 2 * qb + h
                    act.wait_ge(max_ready, it * SCORES + i + 1)
                    act.activation(probs[:, h, qb % 2, 0:P * (qb + 1)], pair[h][:, columns_of(qb)], ACT.Exp,
                                   bias=neg_max[:, i:i + 1], accum_out=row_sum[:, i:i + 1]).then_inc(probs_ready, 1)

                def keep_flip(it, qb, h):
                    g, key0 = group(qb)
                    lo = 0 if g == 0 else GB
                    act.wait_ge(flipped1, it * FLIPS + flips_before(qb) + (h if g else 0) + 1)
                    at = P * (qb % GB)
                    act.activation(probs_T[:, h, key0 + lo:key0 + qb + 1, at:at + P],
                                   flip[1][:, 0:P * (qb + 1 - lo)].rearrange("p (k q) -> p k q", q=P),
                                   ACT.Copy).then_inc(flip1_kept, 1)

                def keep_recip(it, g):
                    act.wait_ge(recip_flipped, it * QG + g + 1 + CREDIT)
                    act.wait_ge(att_kept, it * QG + g + CREDIT)
                    act.activation(recip_T[:], misc[:], ACT.Copy).then_inc(recipT_kept, 1)

                def begin(it):
                    for qb in range(2):
                        for h in range(2):
                            softmax(it, qb, h)

                def unit(it, n, more):
                    for qb in range(2):
                        keep_flip(it, qb, 1)
                        for h in range(2):
                            softmax(it, qb + 2, h)
                    keep_flip(it, 2, 1)
                    for h in range(2):
                        softmax(it, 4, h)
                    keep_flip(it, 3, 1)
                    for h in range(2):
                        softmax(it, 5, h)
                    keep_recip(it, 0)
                    for qb in range(4, ROWS - 2):
                        for h in range(2):
                            keep_flip(it, qb, h)
                            softmax(it, qb + 2, h)
                    for qb in range(ROWS - 2, ROWS):
                        for h in range(2):
                            keep_flip(it, qb, h)
                            if more:
                                keep_part(it + 1, n + 1, h, qb - (ROWS - 2))
                    keep_recip(it, 1)
                    if more:
                        begin(it + 1)

                with act.Fori(0, B) as b:
                    act.wait_ge(xn_flipped1, b + 1 + CREDIT)
                    act.activation(xnT[:, 512:1024], flip[1][:], ACT.Copy).then_inc(xnT_act, 1)
                    for c in range(2):
                        for h in range(2):
                            keep_part(b * PAIRS, 0, h, c)
                    for j in range(NHID):
                        act.wait_ge(gate_ready, b * NHID + j + 1)
                        act.wait_ge(hid_kept, b * NHID + j + CREDIT)
                        act.activation(act_gate[:], pair[0][:], ACT.Silu).then_inc(silu_ready, 1)
                    begin(b * PAIRS)
                    with act.Fori(0, PAIRS - 1) as n:
                        unit(b * PAIRS + n, n, True)
                    unit(b * PAIRS + PAIRS - 1, PAIRS - 1, False)

            @block.vector
            def _(dve):
                dve.sem_inc(flip0_kept, CREDIT)
                dve.sem_inc(att_kept, CREDIT)
                dve.sem_inc(hid_kept, CREDIT)
                dve.sem_inc(x1_kept, CREDIT)
                dve.memset(zero[:], 0.0).then_inc(consts_made, 1)
                dve.memset(scale_row[:], SCALE).then_inc(consts_made, 1)
                with dve.Fori(0, B) as b:
                    dve.wait_ge(x_loaded, 16 * B)
                    rows = [x1[:, bass.ds(b, 1), r, :].rearrange("p a e -> p (a e)") for r in range(ROWS)]
                    for r in range(ROWS):
                        last = dve.bn_stats(stats[:, r, :], rows[r])
                    last.then_inc(dve_step, 1)
                    dve.wait_ge(dve_step, b + 1)
                    dve.memset(eps[:], EPS)
                    for r in range(ROWS):
                        last = dve.bn_aggr(mv[:, r, :], stats[:, r, :])
                    last.then_inc(var_ready, 1)
                    dve.wait_ge(rstd_ready, b + 1)
                    for r in range(ROWS):
                        last = dve.tensor_scalar(xn_all[:, bass.ds(b, 1), r, :].rearrange("p a e -> p (a e)"), rows[r],
                                                 mv[:, r, 0:1], rstd[:, r:r + 1], ALU.subtract, ALU.mult)
                    last.then_inc(xn_ready, 1)
                dve.wait_ge(ints_loaded, 48)
                dve.tensor_scalar(raw_f, raw, INT_SCALE, None, ALU.mult).then_inc(ints_scaled, 1)
                dve.wait_ge(setup_flipped, 1)
                dve.tensor_copy(gate_T[:], pair[0][:, 0:HID]).then_inc(setup_copied, 1)
                dve.tensor_copy(up_T[:], pair[0][:, HID:2 * HID]).then_inc(setup_copied, 1)
                dve.tensor_copy(down_T[:], pair[1][:, 0:HID]).then_inc(setup_copied, 1)
                dve.tensor_copy(columns[:], pair[1][:, 512:512 + COLUMNS]).then_inc(setup_copied, 1)
                dve.wait_ge(setup_copied, 4)
                dve.tensor_scalar(bq8, bq8, SCALE, None, ALU.mult).then_inc(bq_scaled, 1)
                dve.wait_ge(bq_scaled, 1)
                dve.wait_ge(small_loaded, 32)

                def keep_rest(it, n, h, c):
                    dve.wait_ge(hi_kept, 4 * it + 2 * c + h + 1)
                    rows = slice(D, P) if c == 0 else slice(0, P)
                    bias = (bq8, bk)[c]
                    dve.scalar_tensor_tensor((q_st, k_lo)[c][h][rows, :], pair[h][rows, :], bias[rows, bass.ds(2 * n + h, 1)],
                                             (q_st, k_hi)[c][h][rows, :].bitcast(F32), ALU.add, ALU.subtract
                                             ).then_inc(lo_kept, 1)

                def maximum(it, qb, h):
                    i = 2 * qb + h
                    dve.wait_ge(scores_ready, it * SCORES + i + 1)
                    dve.tensor_reduce(out=neg_max[:, i:i + 1], in_=pair[h][:, columns_of(qb)], axis=AX.X,
                                      op=ALU.max, negate=True).then_inc(max_ready, 1)

                def keep_flip(it, qb, h):
                    g, key0 = group(qb)
                    hi = qb + 1 if g == 0 else GB
                    dve.wait_ge(flipped0, it * FLIPS + flips_before(qb) + (h if g else 0) + 1)
                    at = P * (qb % GB)
                    dve.tensor_copy(probs_T[:, h, key0:key0 + hi, at:at + P],
                                    flip[0][:, 0:P * hi].rearrange("p (k q) -> p k q", q=P)).then_inc(flip0_kept, 1)

                def invert(it, g):
                    dve.wait_ge(probs_ready, it * SCORES + 2 * GB * (g + 1) + CREDIT)
                    dve.wait_ge(recip_flipped, it * QG + g + CREDIT)
                    dve.reciprocal(recip[:], row_sum[:, 2 * GB * g:2 * GB * (g + 1)]).then_inc(recip_step, 1)
                    dve.wait_ge(recip_step, it * QG + g + 1)
                    dve.tensor_copy(recip_x[:], recip[:].unsqueeze(2).broadcast_to([P, 2 * GB, D])).then_inc(recip_ready, 1)

                def normalise(it, n, g):
                    dve.wait_ge(recipT_kept, it * QG + g + 1 + CREDIT)
                    dve.wait_ge(pv_ready, it * QG + g + 1)
                    dve.tensor_tensor(att_T[:, bass.ds(n, 1), 512 * g:512 * (g + 1)].rearrange("p a q -> p (a q)"),
                                      accum[:], recip_T[:], ALU.mult).then_inc(att_kept, 1)

                def first_maxima(it):
                    for qb in range(2):
                        for h in range(2):
                            maximum(it, qb, h)

                def keep_values(it, n, half):
                    if half == 0:
                        dve.wait_ge(low_weighed, it + CREDIT)
                    dve.wait_ge(v_made, 2 * it + half + 1 + CREDIT)
                    dve.tensor_tensor(v_sb[:, GB * half:GB * (half + 1), :],
                                      (flip[0], misc)[half][:].rearrange("p (r d) -> p r d", r=GB),
                                      bv_bc[:, bass.ds(n * 2 * D, 2 * D)].unsqueeze(1).broadcast_to([P, GB, 2 * D]),
                                      ALU.add).then_inc(v_kept, 1)

                def unit(it, n, more):
                    for qb in range(2):
                        keep_flip(it, qb, 0)
                        for h in range(2):
                            maximum(it, qb + 2, h)
                    keep_flip(it, 2, 0)
                    maximum(it, 4, 0)
                    keep_flip(it, 3, 0)
                    maximum(it, 4, 1)
                    invert(it, 0)
                    for h in range(2):
                        maximum(it, 5, h)
                    for qb in range(4, ROWS - 2):
                        for h in range(2):
                            keep_flip(it, qb, h)
                            maximum(it, qb + 2, h)
                            if qb == 4 and h == 0:
                                normalise(it, n, 0)
                    for h in range(2):
                        keep_flip(it, ROWS - 2, h)
                    for h in range(2):
                        if more:
                            keep_rest(it + 1, n + 1, h, 0)
                        keep_flip(it, ROWS - 1, h)
                    invert(it, 1)
                    if more:
                        for h in range(2):
                            keep_rest(it + 1, n + 1, h, 1)
                        first_maxima(it + 1)
                        keep_values(it + 1, n + 1, 0)
                    normalise(it, n, 1)
                    if more:
                        keep_values(it + 1, n + 1, 1)

                with dve.Fori(0, B) as b:
                    dve.wait_ge(xn_flipped0, b + 1)
                    dve.tensor_copy(xnT[:, 0:512], flip[0][:]).then_inc(xnT_dve, 1)
                    for c in range(2):
                        for h in range(2):
                            keep_rest(b * PAIRS, 0, h, c)
                    for j in range(NHID):
                        dve.wait_ge(silu_ready, b * NHID + j + 1)
                        dve.wait_ge(up_ready, b * NHID + j + 1)
                        dve.tensor_tensor(hid_T[:, j, :], pair[1][:], act_gate[:], ALU.mult).then_inc(hid_kept, 1)
                    first_maxima(b * PAIRS)
                    for half in range(2):
                        keep_values(b * PAIRS, 0, half)
                    with dve.Fori(0, PAIRS - 1) as n:
                        unit(b * PAIRS + n, n, True)
                    unit(b * PAIRS + PAIRS - 1, PAIRS - 1, False)
                    dve.wait_ge(xob_ready, b + 1)
                    for f in range(2):
                        dve.wait_ge(branch_ready, 2 * b + f + 1)
                        rows = x1[:, bass.ds(b, 1), GB * f:GB * (f + 1), :].rearrange("p a r e -> p (a r e)")
                        dve.tensor_tensor(rows, flip[f][:], rows, ALU.add).then_inc(x1_kept, 1)

            @block.tensor
            def _(pe):
                pe.sem_inc(v_made, CREDIT)
                pe.sem_inc(low_weighed, CREDIT)
                pe.sem_inc(xn_flipped1, CREDIT)
                pe.sem_inc(recip_flipped, CREDIT)
                pe.wait_ge(ident_made, 1)
                pe.wait_ge(ints_scaled, 1)
                pe.wait_ge(stage_loaded, 16 * 7)
                for w in range(2):
                    for j in range(NHID):
                        pe.transpose(pair[0][:, w * HID + j * P:w * HID + (j + 1) * P], raw_f[:, w, j * P:(j + 1) * P], ident[:])
                for j in range(NHID):
                    pe.transpose(pair[1][:, j * P:(j + 1) * P], raw_f[:, 2, j * P:(j + 1) * P], ident[:])
                pe.transpose(pair[1][:, 512:512 + COLUMNS], stage[:], ident[0:COLUMNS, 0:COLUMNS]).then_inc(setup_flipped, 1)
                pe.wait_ge(mask_made, 2)
                pe.wait_ge(setup_copied, 4)

                def project(it, h, c):
                    if c:
                        pe.wait_ge(lo_kept, 4 * it + h + 1)
                    for half in range(2):
                        last = pe.matmul(pair[h][:, 512 * half:512 * (half + 1)],
                                         lhsT=w_qk[:, c, h, :, :].rearrange("p c d -> p (c d)"),
                                         rhs=xnT[:, 512 * half:512 * (half + 1)], start=True, stop=True)
                    last.then_inc(proj_made, 1)

                def project_values(it, half):
                    if half:
                        pe.wait_ge(recipT_kept, it * QG + CREDIT)
                    for r in range(GB):
                        last = pe.matmul((flip[0], misc)[half][:, P * r:P * (r + 1)],
                                         lhsT=xnT[:, P * (GB * half + r):P * (GB * half + r + 1)],
                                         rhs=w_v[:].rearrange("p h d -> p (h d)"), start=True, stop=True)
                    last.then_inc(v_made, 1)

                def score(it, qb, h):
                    if qb < 2:
                        pe.wait_ge(lo_kept, 4 * it + 2 + h + 1)
                    elif qb < GB:
                        pe.wait_ge(probs_ready, it * SCORES + 2 * (qb - 2) + h + 1 + CREDIT)
                    else:
                        pe.wait_ge(probs_ready, it * SCORES + 2 * (qb - 1) + h + 1 + CREDIT)
                    L = P * (qb + 1)
                    at = columns_of(qb).start
                    for lo in range(0, L, 512):
                        w = max(2 * P, min(512, L - lo))
                        for k, part in enumerate((k_hi, k_lo)):
                            pe.matmul(pair[h][:, at + lo:at + lo + w], lhsT=q_st[h][:, P * qb:P * (qb + 1)],
                                      rhs=part[h][:, lo:lo + w], start=k == 0, stop=k == 1 and lo + 512 < L)
                    pe.matmul(pair[h][:, at + L - P:at + L], lhsT=ident_bf[:], rhs=mask[:], start=False, stop=True
                              ).then_inc(scores_ready, 1)

                def flip_probs(it, qb, h):
                    pe.wait_ge(probs_ready, it * SCORES + 2 * qb + h + 1 + CREDIT)
                    at0 = it * FLIPS + flips_before(qb) + CREDIT
                    todo = [(h, at0, 0, qb + 1)] if qb < GB else [(0, at0 + h, 0, GB), (1, at0 + h, GB, qb + 1)]
                    for f, before, lo, hi in todo:
                        pe.wait_ge((flip0_kept, flip1_kept)[f], before)
                        for k in range(lo, hi):
                            last = pe.transpose(flip[f][:, P * (k - lo):P * (k - lo + 1)],
                                                probs[:, h, qb % 2, P * k:P * (k + 1)], ident[:])
                        last.then_inc((flipped0, flipped1)[f], 1)

                def flip_recip(it, g):
                    pe.wait_ge(recip_ready, it * QG + g + 1)
                    if g == 0:
                        pe.wait_ge(v_kept, 2 * (it + 1))
                    else:
                        pe.wait_ge(recipT_kept, it * QG + 1 + CREDIT)
                    for qb in range(GB):
                        last = pe.transpose(misc[:, P * qb:P * (qb + 1)],
                                            recip_x[:, 2 * qb:2 * qb + 2, :].rearrange("p h d -> p (h d)"), ident[:])
                    last.then_inc(recip_flipped, 1)

                def weigh(it, g, lo, hi):
                    keys, key0 = GB * (g + 1), group(g * GB)[1]
                    if lo == 0:
                        done = it * FLIPS + flips_before(GB * (g + 1)) + CREDIT
                        pe.wait_ge(flip0_kept, done)
                        pe.wait_ge(flip1_kept, done)
                        pe.wait_ge(att_kept, it * QG + g + CREDIT)
                    for k in range(lo, hi):
                        at = P * max(0, k - GB * g)
                        for h in range(2):
                            last = pe.matmul(accum[D * h:D * (h + 1), at:512], lhsT=v_sb[:, k, D * h:D * (h + 1)],
                                             rhs=probs_T[:, h, key0 + k, at:512], start=k == 0, stop=k == keys - 1)
                    if hi == keys:
                        last.then_inc(pv_ready, 1)
                    elif g:
                        last.then_inc(low_weighed, 1)

                def first_scores(it):
                    for qb in range(2):
                        for h in range(2):
                            score(it, qb, h)

                def unit(it, more):
                    pe.wait_ge(v_kept, 2 * it + 1)
                    for qb in range(2):
                        for h in range(2):
                            flip_probs(it, qb, h)
                        for h in range(2):
                            score(it, qb + 2, h)
                    for h in range(2):
                        flip_probs(it, 2, h)
                    for h in range(2):
                        score(it, 4, h)
                        flip_probs(it, 3, h)
                    score(it, 5, 0)
                    weigh(it, 0, 0, GB)
                    score(it, 5, 1)
                    flip_recip(it, 0)
                    for qb in range(4, ROWS - 2):
                        for h in range(2):
                            flip_probs(it, qb, h)
                            score(it, qb + 2, h)
                    if more:
                        pe.wait_ge(q_scaled, it + 2)
                    for h in range(2):
                        flip_probs(it, ROWS - 2, h)
                        if more:
                            pe.wait_ge(probs_ready, it * SCORES + 2 * (ROWS - 1) + h + 1 + CREDIT)
                            project(it + 1, h, 0)
                    for h in range(2):
                        flip_probs(it, ROWS - 1, h)
                        if more:
                            project(it + 1, h, 1)
                    weigh(it, 1, 0, GB)
                    flip_recip(it, 1)
                    if more:
                        first_scores(it + 1)
                        project_values(it + 1, 0)
                    weigh(it, 1, GB, 2 * GB)
                    if more:
                        project_values(it + 1, 1)

                with pe.Fori(0, B) as b:
                    pe.wait_ge(xn_placed, b + 1)
                    pe.wait_ge(x1_kept, 2 * b + CREDIT)
                    for r in range(ROWS):
                        last = pe.transpose(flip[r // GB][:, P * (r % GB):P * (r % GB + 1)], xn[:, r, :], ident[:])
                        if r == GB - 1:
                            last.then_inc(xn_flipped0, 1)
                    last.then_inc(xn_flipped1, 1)
                    pe.wait_ge(xnT_dve, b + 1)
                    pe.wait_ge(xnT_act, b + 1)
                    pe.wait_ge(q_scaled, b * PAIRS + 1)
                    for c in range(2):
                        for h in range(2):
                            project(b * PAIRS, h, c)
                    for j in range(NHID):
                        for h, w_T in enumerate((gate_T, up_T)):
                            if j == 0:
                                pe.wait_ge(lo_kept, 4 * PAIRS * b + 2 + h + 1)
                            elif h == 0:
                                pe.wait_ge(silu_ready, b * NHID + j)
                            else:
                                pe.wait_ge(hid_kept, b * NHID + j + CREDIT)
                            for half in range(2):
                                last = pe.matmul(pair[h][:, 512 * half:512 * (half + 1)], lhsT=w_T[:, P * j:P * (j + 1)],
                                                 rhs=xnT[:, 512 * half:512 * (half + 1)], start=True, stop=True)
                            last.then_inc((gate_ready, up_ready)[h], 1)
                    pe.wait_ge(silu_ready, (b + 1) * NHID)
                    pe.wait_ge(hid_kept, (b + 1) * NHID + CREDIT)
                    first_scores(b * PAIRS)
                    for half in range(2):
                        project_values(b * PAIRS, half)
                    with pe.Fori(0, PAIRS - 1) as n:
                        unit(b * PAIRS + n, True)
                    unit(b * PAIRS + PAIRS - 1, False)
                    pe.wait_ge(outw_loaded, 16)
                    pe.wait_ge(att_kept, (b + 1) * PAIRS * QG + CREDIT)
                    for r in range(ROWS):
                        dst = flip[r // GB][:, P * (r % GB):P * (r % GB + 1)]
                        for n2 in range(PAIRS):
                            pe.matmul(dst, lhsT=att_T[:, n2, P * r:P * (r + 1)], rhs=outw_sb[:, n2, :], start=n2 == 0, stop=False)
                        for j in range(NHID):
                            last = pe.matmul(dst, lhsT=hid_T[:, j, P * r:P * (r + 1)], rhs=down_T[:, P * j:P * (j + 1)],
                                             start=False, stop=j == NHID - 1)
                        if r % GB == GB - 1:
                            last.then_inc(branch_ready, 1)


def layer1(nc, sem, sbuf, kept, W1, W2, late, out):
    pair, flip, accum, misc, x1, ident, columns, minus_half, eps = kept
    slow_sb, beta_w, wout_sb, wg_sb, b2_sb, late_loaded = late
    b1_col, lnw_col, lnb_col = columns[:, 2 * H:2 * H + X * NXB], columns[:, COLUMNS - 2:COLUMNS - 1], columns[:, COLUMNS - 1:COLUMNS]
    HD = H * D
    PARTS = 3 * B
    XS = X // B
    PRODS = 2 * B - 1
    SUMS = B - 1
    STEPS = SUMS * (SUMS + 1) // 2 - SUMS
    HALVES = 2 * B
    ctx = ExitStack()
    with ctx:
        def sb(name, shape, dt=F32):
            return sbuf(name, shape, dt, ctx)

        w1_sb = sb("w1_sb", [P, X, XH])
        w2_sb = sb("w2_sb", [P, X, NXB, E])
        experts_loaded = sem("experts_loaded")
        stats1 = sb("stats1", [P, B, 6])
        mv_n, mv_h = sb("mv_n", [P, B, 2]), sb("mv_h", [P, B, 2])
        rstd_n, rstd_h = sb("rstd_n", [P, B]), sb("rstd_h", [P, B])
        nrm = sb("nrm", [P, B, E])
        hat = sb("hat", [P, B, E])
        nrm_T = sb("nrm_T", [P, B * P])
        h_T = sb("h_T", [P, B * P])
        small = sb("small", [P, B * (H + X)])
        sig = sb("sig", [P, 2, B * H])
        beta = sb("beta", [P, B, H])
        gate = sb("gate", [P, B, X])
        stat4 = sb("stat4", [P, 4, B])
        above = sb("above", [P, B, X, X])
        equal = sb("equal", [P, B, X, X])
        earlier = sb("earlier", [P, X, X])
        rank = sb("rank", [P, B, X])
        score = sb("score", [P, B, X])
        score_T = sb("score_T", [X, B * P])
        e_buf = sb("e_buf", [P, 2, HD])
        qs = sb("qs", [P, 2, HD])
        ks = sb("ks", [P, B, HD])
        vs = sb("vs", [P, B, HD])
        v_next = sb("v_next", [P, HD])
        inv_qk = sb("inv_qk", [P, B, 2, H])
        decay = sb("decay", [P, B, H])
        prod = [sb("prod0", [P, 2 * B - 3, HD]), sb("prod1", [P, 2 * B - 1, HD])]
        kk = sb("kk", [P, B, H])
        qk = sb("qk", [P, B, H])
        U = sb("U", [P, B, B, H])
        tmp = sb("tmp", [P, B, B, H])
        M = sb("M", [P, B, H])
        terms = [sb("terms0", [P, B - 1, HD]), sb("terms1", [P, B, HD])]
        outs_T = sb("outs_T", [P, PAIRS, P])
        hid = sb("hid", [P, 2, NXB, B * P])

        earlier_step, earlier_made = sem("earlier_step"), sem("earlier_made")
        u_cleared, norm_step, gate_step, row_step = sem("u_cleared"), sem("norm_step"), sem("gate_step"), sem("row_step")
        inv_step, varn_step = sem("inv_step"), sem("varn_step")
        varn_ready, rstdn_ready, varh_ready, rstdh_ready = sem("varn_ready"), sem("rstdn_ready"), sem("varh_ready"), sem("rstdh_ready")
        nrm_ready, hat_ready, resid_ready = sem("nrm_ready"), sem("hat_ready"), sem("resid_ready")
        nrm_flipped, hat_flipped, nrmT_kept, hT_kept = sem("nrm_flipped"), sem("hat_flipped"), sem("nrmT_kept"), sem("hT_kept")
        small_made, small_kept, beta_low, beta_exp = sem("small_made"), sem("small_kept"), sem("beta_low"), sem("beta_exp")
        logit_ready, gate_exp = sem("logit_ready"), sem("gate_exp_l1")
        score_ready, score_flipped, scoreT_kept = sem("score_ready"), sem("score_flipped"), sem("scoreT_kept")
        part_ready, low_ready, e_ready = sem("part_ready"), sem("low_ready"), sem("e_ready")
        qk_kept, vs_kept, v0_placed = sem("qk_kept"), sem("vs_kept"), sem("v0_placed")
        hid_ready, hid_kept = sem("hid_ready"), sem("hid_kept_l1")
        y_ready, y_kept = sem("y_ready"), sem("y_kept")
        prod_ready, prod_used = sem("prod_ready"), sem("prod_used")
        terms_ready, sum_step, sum_ready = sem("terms_ready"), sem("sum_step"), sem("sum_ready")
        out_flipped, outT_kept = sem("out_flipped"), sem("outT_kept")
        attn_ready, fin_ready, stored = sem("attn_ready"), sem("fin_ready"), sem("stored")

        out_v = out.rearrange("s (t p) e -> t p s e", p=P)

        def heads(ap):
            return ap.rearrange("p (h d) -> p h d", h=H)

        def rows_of(t):
            return x1[:, :, bass.ds(t, 1), :].rearrange("p s a e -> p s (a e)")

        def row_of(t, s):
            return x1[:, s, bass.ds(t, 1), :].rearrange("p a e -> p (a e)")

        def tiles(engine, body):
            body(0, True, False)
            with engine.Fori(1, ROWS - 1) as t:
                body(t, False, False)
            body(ROWS - 1, False, True)

        with nc.Block() as block:

            @block.sync
            def _(sp):
                sp.dma_start(w1_sb[:], W1.rearrange("x e h -> e x h")).then_inc(experts_loaded, 16)
                sp.dma_start(w2_sb[:], W2.rearrange("x (j p) e -> p x j e", p=P)).then_inc(experts_loaded, 16)
                with sp.Fori(0, ROWS) as t:
                    sp.wait_ge(fin_ready, t + 1)
                    sp.dma_start(out_v[t], rows_of(t)).then_inc(stored, 16)
                sp.wait_ge(stored, 16 * ROWS)

            @block.gpsimd
            def _(pool):
                pool.memset(earlier[:], 1.0).then_inc(earlier_step, 1)
                pool.wait_ge(earlier_step, 1)
                pool.affine_select(out=earlier[:], in_=earlier[:], compare_op=ALU.is_gt, fill=0.0, base=0,
                                   pattern=[[1, X], [-1, X]], channel_multiplier=0).then_inc(earlier_made, 1)

                def deviation(t, mv, rstd, ready, step, done):
                    pool.wait_ge(ready, t + 1)
                    pool.tensor_tensor(rstd[:], mv[:, :, 1], eps[:, 0:B], ALU.add).then_inc(varn_step, 1)
                    pool.wait_ge(varn_step, 2 * t + step)
                    pool.tensor_tensor(rstd[:], rstd[:], minus_half[:, 0:B], ALU.pow).then_inc(done, 1)

                def norm_deviation(t):
                    deviation(t, mv_n, rstd_n, varn_ready, 1, rstdn_ready)

                def hat_deviation(t):
                    deviation(t, mv_h, rstd_h, varh_ready, 2, rstdh_ready)

                def residual(t):
                    pool.wait_ge(nrm_ready, t + 1)
                    pool.wait_ge(earlier_made, 1)
                    pool.tensor_tensor(rows_of(t), nrm[:], rows_of(t), ALU.add).then_inc(resid_ready, 1)

                def products(t, s, first):
                    dst = prod[s % 2]
                    pool.wait_ge(qk_kept, 2 * (B * t + s + 1))
                    if s >= 2 or not first:
                        pool.wait_ge(prod_used, B * t + s - 1)
                    if s:
                        pool.tensor_tensor(dst[:, 0:s, :], ks[:, 0:s, :],
                                           ks[:, s:s + 1, :].broadcast_to([P, s, HD]), ALU.mult).then_inc(prod_ready, 1)
                    pool.tensor_tensor(dst[:, s:2 * s + 1, :], ks[:, 0:s + 1, :],
                                       qs[:, s % 2:s % 2 + 1, :].broadcast_to([P, s + 1, HD]), ALU.mult).then_inc(prod_ready, 1)

                def sums(t, r):
                    pool.wait_ge(terms_ready, B * t + r + 1)
                    rows = terms[r % 2]
                    for k in range(1, r + 1):
                        if k > 1:
                            pool.wait_ge(sum_step, STEPS * t + (r - 1) * (r - 2) // 2 + k - 1)
                        pool.tensor_tensor(rows[:, 0, :], rows[:, 0, :], rows[:, k, :], ALU.add
                                           ).then_inc(sum_ready if k == r else sum_step, 1)

                def tile(t, first, last):
                    if not first:
                        sums(t - 1, 2)
                    products(t, 0, first)
                    if not first:
                        sums(t - 1, 3)
                    if not last:
                        norm_deviation(t + 1)
                    products(t, 1, first)
                    products(t, 2, first)
                    if not last:
                        hat_deviation(t + 1)
                    sums(t, 1)
                    products(t, 3, first)
                    if not last:
                        residual(t + 1)

                norm_deviation(0)
                hat_deviation(0)
                residual(0)
                tiles(pool, tile)
                sums(ROWS - 1, 2)
                sums(ROWS - 1, 3)

            @block.scalar
            def _(act):
                def begin(t):
                    act.wait_ge(nrm_flipped, t + 1)
                    act.activation(nrm_T[:], flip[0][:], ACT.Copy).then_inc(nrmT_kept, 1)
                    act.wait_ge(hat_flipped, t + 1)
                    act.activation(h_T[:], flip[1][:], ACT.Identity, bias=lnb_col, scale=lnw_col).then_inc(hT_kept, 1)
                    act.wait_ge(small_made, t + 1)
                    act.activation(small[:], flip[0][:, 0:B * (H + X)], ACT.Copy).then_inc(small_kept, 1)
                    act.wait_ge(small_kept, t + 1)
                    act.activation(sig[:, 0, :], small[:, 0:B * H], ACT.Relu, scale=-1.0).then_inc(beta_low, 1)
                    act.activation(sig[:, 1, :], small[:, 0:B * H], ACT.Abs).then_inc(beta_low, 1)
                    act.wait_ge(beta_low, 2 * t + 2)
                    act.activation(sig[:], sig[:], ACT.Exp, scale=-1.0).then_inc(beta_exp, 1)

                def gates(t):
                    act.wait_ge(logit_ready, t + 1)
                    act.activation(gate[:], gate[:], ACT.Exp).then_inc(gate_exp, 1)

                def exps(t, s, first):
                    for k in range(2):
                        act.wait_ge(part_ready, PARTS * t + 3 * s + k + 1)
                        if s or not first:
                            act.wait_ge(qk_kept, 2 * (B * t + s - 1) + k + 1)
                        act.activation(e_buf[:, k, :], pair[(3 * s + k) % 2][:], ACT.Relu, scale=-1.0).then_inc(low_ready, 1)
                        act.wait_ge(low_ready, 2 * (B * t + s) + k + 1)
                        act.activation(e_buf[:, k, :], e_buf[:, k, :], ACT.Exp, scale=-1.0).then_inc(e_ready, 1)

                def keep_values(t, s, first):
                    act.wait_ge(part_ready, PARTS * t + 3 * s + 3)
                    if s == 1 and not first:
                        act.wait_ge(terms_ready, B * t)
                    act.activation(vs[:, s, :] if s else v_next[:], pair[(3 * s + 2) % 2][:], ACT.Copy).then_inc(vs_kept, 1)
                    if s == 1:
                        act.wait_ge(vs_kept, B * t + 1)
                        act.activation(vs[:, 0, :], v_next[:], ACT.Copy).then_inc(v0_placed, 1)

                def relus(t, e, first):
                    for j in range(NXB):
                        act.wait_ge(hid_ready, X * NXB * t + NXB * e + j + 1)
                        if e >= 2 or not first:
                            act.wait_ge(y_ready, X * t + e - 1)
                        act.activation(hid[:, e % 2, j, :], flip[j][:], ACT.Relu,
                                       bias=b1_col[:, NXB * e + j:NXB * e + j + 1]).then_inc(hid_kept, 1)

                def keep_out(t, r):
                    for j in range(2):
                        act.wait_ge(out_flipped, HALVES * t + 2 * r + j + 1)
                        act.activation(outs_T[:, PAIRS // 2 * j:PAIRS // 2 * (j + 1), :].rearrange("p n q -> p (n q)"),
                                       flip[j][:], ACT.Copy).then_inc(outT_kept, 1)

                def keep_scores(t, first):
                    act.wait_ge(score_flipped, t + 1)
                    if not first:
                        act.wait_ge(attn_ready, t)
                    act.activation(score_T[:], flip[1][0:X, :], ACT.Copy).then_inc(scoreT_kept, 1)

                def tile(t, first, last):
                    for s in range(B):
                        keep_values(t, s, first)
                        if s < B - 1:
                            exps(t, s + 1, first)
                            relus(t, XS * (s + 1), first)
                        if s == 2:
                            keep_scores(t, first)
                        if s >= 2:
                            keep_out(t, s - 2)
                        elif not first:
                            keep_out(t - 1, s + 2)
                        if s < B - 1:
                            relus(t, XS * (s + 1) + 1, first)
                    if not last:
                        begin(t + 1)
                        exps(t + 1, 0, False)
                        for e in range(XS):
                            relus(t + 1, e, False)
                        gates(t + 1)

                begin(0)
                exps(0, 0, True)
                for e in range(XS):
                    relus(0, e, True)
                gates(0)
                tiles(act, tile)
                for r in range(2, B):
                    keep_out(ROWS - 1, r)

            @block.vector
            def _(dve):
                dve.memset(U[:], 0.0).then_inc(u_cleared, 1)
                dve.wait_ge(u_cleared, 1)

                def links(done, steps, t, total, before):
                    count = [0]

                    def link(op):
                        op.then_inc(done, 1)
                        count[0] += 1
                        assert count[0] <= steps
                        dve.wait_ge(done, total * t + before + count[0])
                    return link

                def statistics(src, mv, step, ready, t):
                    for s in range(B):
                        last = dve.bn_stats(stats1[:, s, :], src(s))
                    last.then_inc(norm_step, 1)
                    dve.wait_ge(norm_step, 2 * t + step)
                    dve.memset(eps[:, 0:B], EPS)
                    for s in range(B):
                        last = dve.bn_aggr(mv[:, s, :], stats1[:, s, :])
                    last.then_inc(ready, 1)

                def normalise(src, dst, mv, rstd, rstd_ready, done, t):
                    dve.wait_ge(rstd_ready, t + 1)
                    for s in range(B):
                        last = dve.tensor_scalar(dst[:, s, :], src(s), mv[:, s, 0:1], rstd[:, s:s + 1],
                                                 ALU.subtract, ALU.mult)
                    last.then_inc(done, 1)

                def norm_statistics(t):
                    statistics(lambda s: row_of(t, s), mv_n, 1, varn_ready, t)

                def norm(t):
                    normalise(lambda s: row_of(t, s), nrm, mv_n, rstd_n, rstdn_ready, nrm_ready, t)
                    dve.wait_ge(nrm_ready, t + 1)
                    statistics(lambda s: nrm[:, s, :], mv_h, 2, varh_ready, t)

                def norm_of_norm(t):
                    normalise(lambda s: nrm[:, s, :], hat, mv_h, rstd_h, rstdh_ready, hat_ready, t)

                GATES, LINKS = 14, (2, 5, 6, 6)

                def over(ap):
                    return ap.unsqueeze(2).broadcast_to([P, B, X])

                def logits(t):
                    link = links(gate_step, 4, t, GATES, 0)
                    mx = stat4[:, 0, :]
                    z = small[:, B * H:B * (H + X)].rearrange("p (s x) -> p s x", s=B)
                    dve.wait_ge(small_kept, t + 1)
                    link(dve.tensor_reduce(out=mx, in_=z, axis=AX.X, op=ALU.max))
                    dve.tensor_tensor(gate[:], z, over(mx), ALU.subtract).then_inc(logit_ready, 1)
                    dve.wait_ge(beta_exp, t + 1)
                    link(dve.tensor_scalar(sig[:, 1, :], sig[:, 1, :], 1.0, None, ALU.add))
                    link(dve.reciprocal(sig[:, 1, :], sig[:, 1, :]))
                    link(dve.tensor_tensor(beta[:].rearrange("p s h -> p (s h)"), sig[:, 0, :], sig[:, 1, :], ALU.mult))

                def gates(t):
                    link = links(gate_step, GATES - 4, t, GATES, 4)
                    total, top_sum, inv = (stat4[:, k, :] for k in range(1, 4))
                    dve.wait_ge(gate_exp, t + 1)
                    link(dve.tensor_reduce(out=total, in_=gate[:], axis=AX.X, op=ALU.add))
                    link(dve.reciprocal(inv, total))
                    link(dve.tensor_tensor(gate[:], gate[:], over(inv), ALU.mult))
                    mine = gate[:].unsqueeze(3).broadcast_to([P, B, X, X])
                    other = gate[:].unsqueeze(2).broadcast_to([P, B, X, X])
                    dve.tensor_tensor(above[:], other, mine, ALU.is_gt)
                    link(dve.tensor_tensor(equal[:], other, mine, ALU.is_equal))
                    dve.wait_ge(earlier_made, 1)
                    link(dve.tensor_tensor(equal[:], equal[:], earlier[:].unsqueeze(1).broadcast_to([P, B, X, X]), ALU.mult))
                    link(dve.tensor_tensor(above[:], above[:], equal[:], ALU.add))
                    link(dve.tensor_reduce(out=rank[:], in_=above[:], axis=AX.X, op=ALU.add))
                    link(dve.scalar_tensor_tensor(rank[:], rank[:], float(TOP), gate[:], ALU.is_lt, ALU.mult))
                    link(dve.tensor_reduce(out=top_sum, in_=rank[:], axis=AX.X, op=ALU.add))
                    link(dve.reciprocal(inv, top_sum))
                    dve.tensor_tensor(score[:], rank[:], over(inv), ALU.mult).then_inc(score_ready, 1)
                    dve.wait_ge(score_ready, t + 1)

                def keep(t, s, first):
                    for k, dst in enumerate((qs[:, s % 2, :], ks[:, s, :])):
                        if s == 0 and k == 1 and not first:
                            dve.wait_ge(prod_ready, PRODS * t)
                        dve.wait_ge(e_ready, 2 * (B * t + s) + k + 1)
                        dve.scalar_tensor_tensor(dst, pair[(3 * s + k) % 2][:], 0.0, e_buf[:, k, :],
                                                 ALU.max, ALU.add).then_inc(qk_kept, 1)

                def invert(t, s):
                    base = 3 * (B * t + s)
                    dve.wait_ge(qk_kept, 2 * (B * t + s + 1))
                    dve.tensor_reduce(out=inv_qk[:, s, 0, :], in_=heads(qs[:, s % 2, :]), axis=AX.X, op=ALU.add)
                    dve.tensor_reduce(out=inv_qk[:, s, 1, :], in_=heads(ks[:, s, :]), axis=AX.X, op=ALU.add).then_inc(inv_step, 1)
                    dve.wait_ge(inv_step, base + 1)
                    dve.reciprocal(inv_qk[:, s, :, :], inv_qk[:, s, :, :]).then_inc(inv_step, 1)
                    dve.wait_ge(inv_step, base + 2)
                    dve.tensor_tensor(U[:, s, s, :], inv_qk[:, s, 1, :], beta[:, s, :], ALU.mult).then_inc(inv_step, 1)
                    dve.wait_ge(inv_step, base + 3)
                    dve.scalar_tensor_tensor(decay[:, s, :], inv_qk[:, s, 1, :], -1.0, U[:, s, s, :], ALU.mult, ALU.mult)

                def gather(t, e):
                    dve.wait_ge(y_ready, X * t + e + 1)
                    if e == 0:
                        dve.wait_ge(resid_ready, t + 1)
                    for s in range(B):
                        last = dve.scalar_tensor_tensor(row_of(t, s), accum[:, P * s:P * (s + 1)], score[:, s, e:e + 1],
                                                        row_of(t, s), ALU.mult, ALU.add)
                    last.then_inc(y_kept, 1)

                def sum_products(t, r):
                    src = prod[r % 2]
                    dve.wait_ge(prod_ready, PRODS * t + 2 * r + 1)
                    if r:
                        dve.tensor_reduce(out=kk[:, 0:r, :], in_=src[:, 0:r, :].rearrange("p s (h d) -> p s h d", h=H),
                                          axis=AX.X, op=ALU.add)
                    dve.tensor_reduce(out=qk[:, 0:r + 1, :], in_=src[:, r:2 * r + 1, :].rearrange("p s (h d) -> p s h d", h=H),
                                      axis=AX.X, op=ALU.add).then_inc(prod_used, 1)

                def mixing(t, r):
                    link = links(row_step, LINKS[r], t, sum(LINKS), sum(LINKS[:r]))
                    dve.wait_ge(prod_used, B * t + r + 1)
                    if r:
                        link(dve.tensor_tensor(tmp[:, 0:r, 0:r, :], U[:, 0:r, 0:r, :],
                                               kk[:, 0:r, :].unsqueeze(2).broadcast_to([P, r, r, H]), ALU.mult))
                        if r > 1:
                            link(dve.tensor_reduce(out=U[:, r, 0:r, :], in_=tmp[:, 0:r, 0:r, :].rearrange("p s u h -> p u h s"),
                                                   axis=AX.X, op=ALU.add))
                        link(dve.tensor_tensor(U[:, r, 0:r, :], U[:, r, 0:r, :] if r > 1 else tmp[:, 0, 0:1, :],
                                               decay[:, r:r + 1, :].broadcast_to([P, r, H]), ALU.mult))
                    n = r + 1
                    link(dve.tensor_tensor(tmp[:, 0:n, 0:n, :], U[:, 0:n, 0:n, :],
                                           qk[:, 0:n, :].unsqueeze(2).broadcast_to([P, n, n, H]), ALU.mult))
                    if r:
                        link(dve.tensor_reduce(out=M[:, 0:n, :], in_=tmp[:, 0:n, 0:n, :].rearrange("p s u h -> p u h s"),
                                               axis=AX.X, op=ALU.add))
                    link(dve.tensor_tensor(M[:, 0:n, :], M[:, 0:n, :] if r else tmp[:, 0, 0:1, :],
                                           inv_qk[:, r, 0:1, :].broadcast_to([P, n, H]), ALU.mult))

                def row(t, r, first):
                    n = r + 1
                    dve.wait_ge(v0_placed, t + 1)
                    dve.wait_ge(vs_kept, B * t + max(n, 2))
                    if r >= 2 or not first:
                        dve.wait_ge(out_flipped, HALVES * t + 2 * (r - 1))
                    dve.tensor_tensor(terms[r % 2][:, 0:n, :].rearrange("p s (h d) -> p (s h) d", h=H),
                                      vs[:, 0:n, :].rearrange("p s (h d) -> p (s h) d", h=H),
                                      M[:, 0:n, :].rearrange("p s h -> p (s h)").unsqueeze(2).broadcast_to([P, n * H, D]),
                                      ALU.mult).then_inc(terms_ready, 1)

                def finish(t):
                    dve.wait_ge(y_kept, X * (t + 1))
                    dve.wait_ge(attn_ready, t + 1)
                    dve.tensor_tensor(rows_of(t), misc[:].rearrange("p (s e) -> p s e", s=B), rows_of(t), ALU.add
                                      ).then_inc(fin_ready, 1)

                def tile(t, first, last):
                    for s in range(B):
                        if s:
                            keep(t, s, first)
                        gather(t, XS * s)
                        if s == 0 and not first:
                            sum_products(t - 1, B - 1)
                            gather(t, 1)
                            mixing(t - 1, B - 1)
                            row(t - 1, B - 1, False)
                        if s == 2 and not first:
                            finish(t - 1)
                        if s == 3 and not last:
                            norm_of_norm(t + 1)
                        if (s == 0 and first) or (s == 1 and not first):
                            invert(t, 0)
                        if s:
                            invert(t, s)
                        if s == 1 and not last:
                            norm_statistics(t + 1)
                        if s:
                            sum_products(t, s - 1)
                        if s or first:
                            gather(t, XS * s + 1)
                        if s == 2 and not last:
                            norm(t + 1)
                        if s:
                            mixing(t, s - 1)
                            row(t, s - 1, first)
                    if not last:
                        logits(t + 1)
                        keep(t + 1, 0, False)
                        gates(t + 1)

                norm_statistics(0)
                norm(0)
                norm_of_norm(0)
                logits(0)
                keep(0, 0, True)
                gates(0)
                tiles(dve, tile)
                sum_products(ROWS - 1, B - 1)
                mixing(ROWS - 1, B - 1)
                row(ROWS - 1, B - 1, False)
                finish(ROWS - 1)

            @block.tensor
            def _(pe):
                pe.wait_ge(late_loaded, 16 * 7)
                pe.wait_ge(experts_loaded, 32)

                def begin(t, very_first):
                    pe.wait_ge(nrm_ready, t + 1)
                    if not very_first:
                        pe.wait_ge(outT_kept, HALVES * (t - 1) + 3)
                    for s in range(B):
                        last = pe.transpose(flip[0][:, P * s:P * (s + 1)], nrm[:, s, :], ident[:])
                    last.then_inc(nrm_flipped, 1)
                    pe.wait_ge(hat_ready, t + 1)
                    if not very_first:
                        pe.wait_ge(outT_kept, HALVES * (t - 1) + 4)
                    for s in range(B):
                        last = pe.transpose(flip[1][:, P * s:P * (s + 1)], hat[:, s, :], ident[:])
                    last.then_inc(hat_flipped, 1)
                    pe.wait_ge(nrmT_kept, t + 1)
                    for s in range(B):
                        pe.matmul(flip[0][:, B * H + X * s:B * H + X * (s + 1)], lhsT=nrm_T[:, P * s:P * (s + 1)], rhs=wg_sb[:],
                                  start=True, stop=True)
                    pe.wait_ge(hT_kept, t + 1)
                    for s in range(B):
                        last = pe.matmul(flip[0][:, H * s:H * (s + 1)], lhsT=h_T[:, P * s:P * (s + 1)], rhs=beta_w[:],
                                         start=True, stop=True)
                    last.then_inc(small_made, 1)

                def project(t, s, c, first):
                    n = 3 * s + c
                    if c == 2:
                        pe.wait_ge(qk_kept, 2 * (B * t + s) + 1)
                    elif c == 1 and (s or not first):
                        pe.wait_ge(vs_kept, B * t + s)
                    elif c == 0 and (s or not first):
                        pe.wait_ge(qk_kept, 2 * (B * t + s))
                    for half in range(2):
                        last = pe.matmul(pair[n % 2][:, 512 * half:512 * (half + 1)], lhsT=h_T[:, P * s:P * (s + 1)],
                                         rhs=slow_sb[:, c, 512 * half:512 * (half + 1)], start=True, stop=True)
                    last.then_inc(part_ready, 1)

                def hidden(t, e, first):
                    for j in range(NXB):
                        if e == 0:
                            pe.wait_ge((small_kept, hT_kept)[j], t + 1)
                        elif e % XS and (e > 3 * XS or (e > XS and not first)):
                            pe.wait_ge(outT_kept, HALVES * t + 2 * (e // XS - 3) + j + 1)
                        else:
                            pe.wait_ge(hid_kept, X * NXB * t + NXB * (e - 1) + j + 1)
                        pe.matmul(flip[j][:], lhsT=w1_sb[:, e, P * j:P * (j + 1)], rhs=nrm_T[:], start=True,
                                  stop=True).then_inc(hid_ready, 1)

                def expert(t, e, first):
                    pe.wait_ge(hid_kept, X * NXB * t + NXB * (e + 1))
                    if e or not first:
                        pe.wait_ge(y_kept, X * t + e)
                    for s in range(B):
                        for j in range(NXB):
                            last = pe.matmul(accum[:, P * s:P * (s + 1)], lhsT=hid[:, e % 2, j, P * s:P * (s + 1)],
                                             rhs=w2_sb[:, e, j, :], start=j == 0, stop=j == NXB - 1)
                    last.then_inc(y_ready, 1)

                def flip_scores(t):
                    pe.wait_ge(score_ready, t + 1)
                    pe.wait_ge(hid_kept, NXB * (X * t + 3 * XS + 1))
                    for s in range(B):
                        last = pe.transpose(flip[1][0:X, P * s:P * (s + 1)], score[:, s, :], ident[:])
                    last.then_inc(score_flipped, 1)

                def flip_out(t, r, now, slot):
                    if r:
                        pe.wait_ge(sum_ready, SUMS * t + r)
                    else:
                        pe.wait_ge(terms_ready, B * t + 1)
                    for j in range(2):
                        if now is None:
                            pe.wait_ge(outT_kept, HALVES * t + 2 * (r - 1) + j + 1)
                        elif r == 0 and j == 1:
                            pe.wait_ge(scoreT_kept, t + 1)
                        else:
                            pe.wait_ge(hid_kept, X * NXB * now + NXB * min(XS * (slot + 1), X - 1) + j + 1)
                        for n in range(PAIRS // 2):
                            at = P * (PAIRS // 2 * j + n)
                            last = pe.transpose(flip[j][:, P * n:P * (n + 1)], terms[r % 2][:, 0, at:at + P], ident[:])
                        last.then_inc(out_flipped, 1)

                def join(t, r, first):
                    if r == 0:
                        pe.wait_ge(scoreT_kept, t + 1)
                        if not first:
                            pe.wait_ge(fin_ready, t)
                    dst = misc[:, P * r:P * (r + 1)]
                    pe.matmul(dst, lhsT=score_T[:, P * r:P * (r + 1)], rhs=b2_sb[:], start=True, stop=False)
                    pe.wait_ge(outT_kept, HALVES * t + 2 * (r + 1))
                    for n in range(PAIRS):
                        last = pe.matmul(dst, lhsT=outs_T[:, n, :], rhs=wout_sb[:, n, :], start=False, stop=n == PAIRS - 1)
                    if r == B - 1:
                        last.then_inc(attn_ready, 1)

                def start(t, first):
                    for c in range(2):
                        project(t, 0, c, first)
                    for e in range(XS):
                        hidden(t, e, first)
                    expert(t, 0, first)

                def tile(t, first, last):
                    for s in range(B):
                        project(t, s, 2, first)
                        if s < B - 1:
                            for c in range(2):
                                project(t, s + 1, c, first)
                        expert(t, XS * s + 1, first)
                        if s < B - 1:
                            hidden(t, XS * (s + 1), first)
                        if s == 2:
                            flip_scores(t)
                        if s >= 2:
                            flip_out(t, s - 2, t, s)
                        elif not first:
                            flip_out(t - 1, s + 2, t, s)
                        if s < B - 1:
                            hidden(t, XS * (s + 1) + 1, first)
                        if s >= 2:
                            join(t, s - 2, first)
                        elif not first:
                            join(t - 1, s + 2, False)
                        if s < B - 1:
                            expert(t, XS * (s + 1), first)
                    if not last:
                        begin(t + 1, False)
                        start(t + 1, False)

                begin(0, True)
                start(0, True)
                tiles(pe, tile)
                for r in range(2, B):
                    flip_out(ROWS - 1, r, None, None)
                    join(ROWS - 1, r, False)


_INS = ['L0_attn_x', 'L0_attn_qkv_w', 'L0_attn_qkv_b', 'L0_attn_out_w', 'L0_attn_out_b', 'L0_ffn_w_gate', 'L0_ffn_w_up',
        'L0_ffn_w_down', 'L1_attn_ln_w', 'L1_attn_ln_b', 'L1_attn_w_slow', 'L1_attn_w_out', 'L1_ffn_Wg', 'L1_ffn_W1',
        'L1_ffn_b1', 'L1_ffn_W2', 'L1_ffn_b2']


def kernel(**inputs):
    import numpy as np
    import concourse.bacc as bacc
    from concourse.bass_utils import run_bass_kernel_spmd

    nc = bacc.Bacc("TRN2", target_bir_lowering=False, num_devices=1)
    arrays, args = {}, []
    for name in _INS:
        a = np.ascontiguousarray(inputs[name])
        arrays[f"in_{name}"] = a
        args.append(nc.dram_tensor(f"in_{name}", a.shape, mybir.dt.from_np(a.dtype), kind="ExternalInput").ap())
    out = nc.dram_tensor("out_0", (B, S, E), F32, kind="ExternalOutput").ap()
    block_kernel(nc, *args, out)
    r = run_bass_kernel_spmd(nc, [arrays], core_ids=[0])
    return r.results[0]["out_0"]
```
